# Optimizing a Trainium2 kernel written in Bass

```python
import numpy as np
import jax
import jax.numpy as jnp

def _softmax(x, axis=-1):
    return jax.nn.softmax(x, axis=axis)

def _gelu(x):
    return jax.nn.gelu(x, approximate=True)

def _silu(x):
    return jax.nn.silu(x)

def _sigmoid(x):
    return jax.nn.sigmoid(x)

def _layernorm(x, axis=-1, eps=1e-05):
    m = jnp.mean(x, axis=axis, keepdims=True)
    v = jnp.var(x, axis=axis, keepdims=True)
    return (x - m) / jnp.sqrt(v + eps)

def _scatter_add(tgt, idx, src, axis=0):
    return tgt.at[idx].add(src)

def _segment_sum(src, seg, n):
    return jax.ops.segment_sum(src, seg, n)
kernel_name = 'mk_adj_resnorm_d2_adj_r2_6af5ce'

def setup_inputs(seed: int=0):
    np.random.seed(seed)
    _w = jnp.asarray

    def _rec_inputs():
        import jax
        import jax.numpy as jnp
        _gk = jax.random.key(seed)
        x = -0.000929 + 1 * jax.random.normal(jax.random.fold_in(_gk, 1), (8, 2048, 64), jnp.float32)
        _a = jax.random.bernoulli(jax.random.fold_in(_gk, 2), 0.00390625, (8, 2048, 2048))
        _a = jnp.logical_or(_a, jnp.swapaxes(_a, -1, -2))
        _a = jnp.logical_or(_a, jnp.eye(2048, dtype=bool))
        _af = _a.astype(jnp.float32)
        _af = _af * jax.random.uniform(jax.random.fold_in(_gk, 3), (8, 2048, 2048), jnp.float32, 0.05, 1)
        adj = _af
        return (x, adj)
    x, adj = _rec_inputs()

    def _L0_gnn_setup():
        import jax, jax.numpy as jnp
        import numpy as np
        B, N, C, R = (4, 2048, 64, 16)
        EPS = 1e-12
        key = jax.random.key(seed)
        k_x, k_w, k_u = jax.random.split(key, 3)
        x = jax.random.normal(k_x, (B, N, C), dtype=jnp.float32)
        W = jax.random.uniform(k_w, (B, N, N), dtype=jnp.float32)
        U = 0.01 * jax.random.normal(k_u, (N, R), dtype=jnp.float32)
        w_scale = jnp.asarray(1.0, dtype=jnp.float32)
        return {'x': x, 'W': W, 'U': U, 'w_scale': w_scale}
    _L0_gnn_all = _L0_gnn_setup()
    _L0_gnn_in = {k: v for k, v in _L0_gnn_all.items() if k in ('U', 'w_scale')}
    del _L0_gnn_all

    def _L1_gnn_setup():
        import jax, jax.numpy as jnp
        import numpy as np
        B, N, F_IN, F_OUT = (128, 256, 64, 64)
        key = jax.random.key(seed)
        k1, k2, k3, k4 = jax.random.split(key, 4)
        stdv = 1.0 / np.sqrt(F_OUT)
        inp = jax.random.normal(k1, (B, N, F_IN), dtype=jnp.float32)
        adj = jax.random.uniform(k2, (B, N, N), dtype=jnp.float32)
        weight = jax.random.uniform(k3, (F_IN, F_OUT), minval=-stdv, maxval=stdv, dtype=jnp.float32)
        bias = jax.random.uniform(k4, (F_OUT,), minval=-stdv, maxval=stdv, dtype=jnp.float32)
        return {'input': inp, 'adj': adj, 'weight': weight, 'bias': bias}
    _L1_gnn_all = _L1_gnn_setup()
    _L1_gnn_in = {k: v for k, v in _L1_gnn_all.items() if k in ('weight', 'bias')}
    del _L1_gnn_all
    return {'x': x, 'adj': adj, 'L0_gnn_U': _L0_gnn_in['U'], 'L0_gnn_w_scale': _L0_gnn_in['w_scale'], 'L1_gnn_weight': _L1_gnn_in['weight'], 'L1_gnn_bias': _L1_gnn_in['bias']}

def reference(x, adj, L0_gnn_U, L0_gnn_w_scale, L1_gnn_weight, L1_gnn_bias):
    import jax
    import jax.numpy as jnp

    def _L0_gnn_ref(x, W, U, w_scale):
        import jax, jax.numpy as jnp
        import numpy as np
        B, N, C, R = (4, 2048, 64, 16)
        EPS = 1e-12
        Ws = 0.5 * (W + jnp.swapaxes(W, -1, -2))
        A = jax.nn.sigmoid(U @ U.T)
        K = Ws * A[None, :, :]
        deg = jnp.maximum(K.sum(axis=-1), EPS)
        d = jax.lax.rsqrt(deg)
        K = K * d[:, :, None] * d[:, None, :]
        return w_scale * jnp.einsum('bnm,bmc->bnc', K, x)

    def _L1_gnn_ref(input, adj, weight, bias):
        import jax, jax.numpy as jnp
        import numpy as np
        B, N, F_IN, F_OUT = (128, 256, 64, 64)
        support = jnp.einsum('bnf,fo->bno', input, weight)
        out = jnp.einsum('bmn,bmo->bno', adj, support)
        return out + bias
    x = _layernorm(x + _L0_gnn_ref(x, adj, L0_gnn_U, L0_gnn_w_scale), axis=-1)
    x = _layernorm(x + _L1_gnn_ref(x, adj, L1_gnn_weight, L1_gnn_bias), axis=-1)
    return x

_drawn_inputs = setup_inputs


def setup_inputs(seed=0):
    import zlib

    import numpy as np

    out = dict(_drawn_inputs(seed))
    spreads = {}
    factors = {'L0_gnn_U': 64.0}
    for name, (base, spread) in spreads.items():
        noise = np.random.default_rng([zlib.crc32(name.encode()), seed]).standard_normal(out[name].shape)
        drawn = base * np.exp(spread * noise) if base else spread * noise
        out[name] = jnp.asarray(drawn.astype(out[name].dtype))
    for name, factor in factors.items():
        out[name] = (out[name] * factor).astype(out[name].dtype)
    return out
```

```python
from contextlib import ExitStack

import concourse.bass as bass
from concourse import mybir

F32 = mybir.dt.float32
BF16 = mybir.dt.bfloat16
ALU = mybir.AluOpType
ACT = mybir.ActivationFunctionType
AX_X = mybir.AxisListType.X

P = 128
CHUNK = 4
CW = CHUNK * P
DEG_EPS = 1e-12
LN_EPS = 1e-5
PARTS = ((0, 0), (0, 1), (1, 0), (1, 1), (0, 2), (2, 0), (1, 2), (2, 1))
EARLY = 4

DEG_STEPS = 4
N0_STEPS = 11
N1_STEPS = 9


def build_chunks(T):
    return [(j, g, list(range(CHUNK * g, min(CHUNK * g + CHUNK, j + 1)))) for j in range(T) for g in range(j // CHUNK + 1)]


def mix_steps(T):
    out = []
    for g in range(T // CHUNK):
        blocks = range(CHUNK * g, CHUNK * g + CHUNK)
        rows = [(i, [j for j in blocks if j <= i], [j for j in blocks if j > i]) for i in range(T)]
        rows.sort(key=lambda r: 0 if not r[2] else 1 if not r[1] else 2)
        out.append(rows)
    return out


def window_plan(T, chunks, pieces):
    early = [c for c, (j, _, _) in enumerate(chunks) if j < EARLY]
    late = [c for c, (j, _, _) in enumerate(chunks) if j >= EARLY]
    plan, n = [("piece", 0), ("piece", 1), ("turn", 0)], 2
    for c in early:
        plan += [("chunk", c), ("piece", n)]
        n += 1
    upfront, middle, tail = 16, 8, 4
    while n < upfront:
        plan.append(("piece", n))
        n += 1
    for k, c in enumerate(late):
        plan.append(("chunk", c))
        due = upfront + min(k + 1, 16) // 2 if k < 16 else upfront + middle + (k - 15) * (pieces - upfront - middle - tail) // (len(late) - 16)
        while n < due:
            plan.append(("piece", n))
            n += 1
    return plan, n


def graph_layers(nc, x, adj, u, w_scale, weight, bias, out):
    B, N, C = x.shape
    R = u.shape[1]
    T = N // P
    G = T // CHUNK
    chunks = build_chunks(T)
    NCH = len(chunks)
    mix = mix_steps(T)
    turned = [(g, i, tr) for g in range(G) for i, _, tr in mix[g] if tr]
    NTU = len(turned)
    spread_order = list(range(EARLY, T)) + list(range(EARLY))
    pieces = [(m, h) for m in spread_order for h in range(G // 2)]
    NP = len(pieces)
    first_of_row = {}
    for c, (j, _, _) in enumerate(chunks):
        first_of_row.setdefault(j, c)

    adj_rows = adj.rearrange("b (r p) n -> b r p n", p=P)
    x_tiles = x.rearrange("b (t p) c -> b p t c", p=P)
    out_tiles = out.rearrange("b (t p) c -> b p t c", p=P)

    def place(row, par):
        return row if row >= EARLY or par == 0 else T + row

    def loads(row, b, t, n):
        return 16 * (2 * (b if row >= EARLY else t) + n)

    with ExitStack() as ctx:
        def sb(name, shape, dt=F32):
            return ctx.enter_context(nc.sbuf_tensor(name, shape, dt))

        def pb(name, shape, dt=F32):
            return ctx.enter_context(nc.psum_tensor(name, shape, dt))

        def sem(name):
            return ctx.enter_context(nc.semaphore(name))

        rows = sb("rows", [P, T + EARLY, N])
        xs = sb("xs", [P, 2, T, C])
        z = sb("z", [P, T, C])
        u_left = sb("u_left", [P, N], BF16)
        u_right = sb("u_right", [P, N], BF16)
        gate = sb("gate", [P, 2, CW])
        kt = sb("kt", [P, 3, CW])
        yt = sb("yt", [P, 2, CW])
        ut = sb("ut", [P, G // 2, CW])
        sums = sb("sums", [P, CW])
        part_a = sb("part_a", [P, CHUNK, C])
        part_b = sb("part_b", [P, CHUNK, C])
        square = sb("square", [P, CW])
        ident = sb("ident", [P, P])
        ident_b = sb("ident_b", [P, P], BF16)
        ones = sb("ones", [P, 32])
        weight2 = sb("weight2", [P, C])
        bias_b = sb("bias_b", [P, 1, C])
        scale_b = sb("scale_b", [P, 1])
        row_sums = sb("row_sums", [P, T, G])
        row_sum = sb("row_sum", [P, T])
        deg = sb("deg", [P, T])
        deg_root = sb("deg_root", [P, T])
        d = sb("d", [P, T])
        d_out = sb("d_out", [P, T])
        n0_mean = sb("n0_mean", [P, CHUNK])
        n0_var = sb("n0_var", [P, 2, CHUNK])
        n0_root = sb("n0_root", [P, 2, CHUNK])
        n0_inv = sb("n0_inv", [P, CHUNK])
        n1_mean = sb("n1_mean", [P, G // 2, CHUNK])
        n1_var = sb("n1_var", [P, 2, G // 2, CHUNK])
        n1_root = sb("n1_root", [P, 2, G // 2, CHUNK])
        n1_inv = sb("n1_inv", [P, G // 2, CHUNK])
        one = sb("one", [P, 2])

        ps_a = pb("ps_a", [P, 2, CW])
        ps_t = pb("ps_t", [P, 2, CW])
        ps_o = pb("ps_o", [P, 2, CW])
        ps_c = pb("ps_c", [P, CW])
        ps_v = pb("ps_v", [P, CW])

        u_in = rows[:, T + 2, 0:T * R].rearrange("p (t r) -> p t r", r=R)
        u_rest = rows[:, T + 2, 512:512 + T * R].rearrange("p (t r) -> p t r", r=R)
        u_rest2 = rows[:, T + 2, 1024:1024 + T * R].rearrange("p (t r) -> p t r", r=R)
        u_part = rows[:, T + 2, 1536:1536 + 3 * T * R // 2].bitcast(BF16).rearrange("p (s t r) -> p s t r", s=3, r=R)
        u_stack = rows[:, T + 3, :].bitcast(BF16).rearrange("p (e t s r) -> p e t s r", e=2, t=T, r=R)

        adj_in = [sem(f"adj_in{r}") for r in range(T + EARLY)]
        x_in = [sem("x_in0"), sem("x_in1")]
        u_in_done = sem("u_in_done")
        const_in = sem("const_in")
        ident_0 = sem("ident_0")
        ident_1 = sem("ident_1")
        const_set = sem("const_set")
        u_split = sem("u_split")
        u_turned = sem("u_turned")
        u_ready = sem("u_ready")
        gate_ready = sem("gate_ready")
        gate_done = sem("gate_done")
        flip_ready = sem("flip_ready")
        sum_done = sem("sum_done")
        k_done = sem("k_done")
        col_ready = sem("col_ready")
        col_out = sem("col_out")
        col_turned = sem("col_turned")
        deg_step = sem("deg_step")
        root_done = sem("root_done")
        z_ready = sem("z_ready")
        scale_done = sem("scale_done")
        kt_ready = sem("kt_ready")
        kt_done = sem("kt_done")
        kt_used = sem("kt_used")
        y_ready = sem("y_ready")
        y_out = sem("y_out")
        y_turned = sem("y_turned")
        n0_step = sem("n0_step")
        n0_rooted = sem("n0_rooted")
        x1_ready = sem("x1_ready")
        row_used = sem("row_used")
        u_out = sem("u_out")
        f_ready = sem("f_ready")
        n1_step = sem("n1_step")
        n1_rooted = sem("n1_rooted")
        n1_read = sem("n1_read")
        out_ready = sem("out_ready")
        stored = sem("stored")

        block = ctx.enter_context(nc.Block())

        @block.sync
        def _(sp):
            def load_row(b, t, par, row):
                sp.dma_start(rows[:, place(row, par), :], adj_rows[b, row]).then_inc(adj_in[place(row, par)], 16)

            def store(b, par):
                sp.wait_ge(out_ready, 2 * b + 2)
                sp.dma_start(out_tiles[b], xs[:, par]).then_inc(stored, 16)

            def behind_the_mix(b, t, par, spread_before=True, last=False):
                if not last:
                    if spread_before:
                        sp.wait_ge(row_used, T * b)
                    else:
                        sp.wait_ge(u_ready, 2)
                    for row in range(EARLY):
                        load_row(b + 1, t + par, 1 - par, row)
                for g in range(G):
                    sp.wait_ge(y_ready, G * b + g + 1)
                    if g == 1 and spread_before:
                        store(b - 1, 1 - par)
                    if g == 2 and not last:
                        if spread_before:
                            sp.wait_ge(stored, 16 * b)
                        sp.dma_start(xs[:, 1 - par], x_tiles[b + 1]).then_inc(x_in[1 - par], 16)
                    for row in range(CHUNK * g, CHUNK * g + CHUNK):
                        w = (row + 1) * P
                        sp.dma_start(rows[:, place(row, par), 0:w], adj_rows[b, row][:, 0:w]).then_inc(
                            adj_in[place(row, par)], 16)

            def behind_the_spread(b, t, par):
                for n, row in enumerate(spread_order[:T - EARLY]):
                    sp.wait_ge(row_used, T * b + n + 1)
                    load_row(b + 1, t + par, 1 - par, row)

            for row in range(T):
                load_row(0, 0, 0, row)
            sp.dma_start(xs[:, 0], x_tiles[0]).then_inc(x_in[0], 16)
            behind_the_mix(0, 0, 0, spread_before=False)
            behind_the_spread(0, 0, 0)
            with sp.Fori(0, B // 2 - 1) as t:
                behind_the_mix(2 * t + 1, t, 1)
                behind_the_spread(2 * t + 1, t, 1)
                behind_the_mix(2 * t + 2, t + 1, 0)
                behind_the_spread(2 * t + 2, t + 1, 0)
            behind_the_mix(B - 1, B // 2 - 1, 1, last=True)
            store(B - 1, 1)
            sp.wait_ge(stored, 16 * B)

        @block.gpsimd
        def _(pool):
            pool.dma_start(u_in, u.rearrange("(t p) r -> p t r", p=P)).then_inc(u_in_done, 16)
            pool.dma_start(weight2[0:C, :], weight).then_inc(const_in, 16)
            pool.dma_start(weight2[C:2 * C, :], weight).then_inc(const_in, 16)
            pool.dma_start(bias_b[:, 0, :], bias.partition_broadcast(P)).then_inc(const_in, 16)
            pool.dma_start(scale_b[:, :], w_scale.partition_broadcast(P)).then_inc(const_in, 16)
            pool.memset(ident[:, :], 0.0).then_inc(ident_0, 1)
            pool.wait_ge(ident_0, 1)
            pool.affine_select(out=ident[:, :], in_=ident[:, :], compare_op=ALU.not_equal, fill=1.0, base=0,
                               pattern=[[-1, P]], channel_multiplier=1).then_inc(ident_1, 1)

        @block.tensor
        def _(pe):
            def build_chunk(b, t, par, c):
                j, g, blocks = chunks[c]
                w = P * len(blocks)
                buf = c % 2
                if c < 2:
                    if not (isinstance(b, int) and b == 0):
                        pe.wait_ge(y_out, G * b)
                else:
                    pe.wait_ge(gate_done, NCH * b + c - 1)
                pe.matmul(ps_a[:, buf, 0:w], u_left[:, j * P:(j + 1) * P], u_right[:, g * CW:g * CW + w],
                          start=True, stop=True).then_inc(gate_ready, 1)
                if first_of_row[j] == c:
                    pe.wait_ge(adj_in[place(j, par)], loads(j, b, t, 1))
                if c >= 2:
                    pe.wait_ge(sum_done, NCH * b + c - 1)
                for k, i in enumerate(blocks):
                    last = pe.transpose(ps_t[:, buf, k * P:(k + 1) * P],
                                        rows[:, place(i, par), j * P:(j + 1) * P], ident[:, :])
                last.then_inc(flip_ready, 1)

            def column_sums(b, par, j):
                for c, (jj, g, blocks) in enumerate(chunks):
                    w = P * len([i for i in blocks if i < j])
                    if jj != j or not w:
                        continue
                    pe.wait_ge(k_done, NCH * b + c + 1)
                    last = pe.matmul(ps_c[32 * g:32 * g + 32, 0:w], ones[:, :],
                                     rows[:, place(j, par), g * CW:g * CW + w],
                                     start=(j == CHUNK * g + 1), stop=(j == T - 1), skip_group_check=True)
                if j == T - 1:
                    last.then_inc(col_ready, 1)

            def turn_sums(b):
                pe.wait_ge(col_out, 2 * b + 2)
                if not (isinstance(b, int) and b == 0):
                    pe.wait_ge(n0_step, N0_STEPS * G * b)
                for k in range(CHUNK):
                    last = pe.transpose(ps_v[:, k * P:(k + 1) * P], sums[:, k * P:(k + 1) * P], ident[:, :])
                last.then_inc(col_turned, 1)

            def turn_k(b, par, n):
                g, i, tr = turned[n]
                if n < 2:
                    pe.wait_ge(k_done, NCH * b + NCH)
                else:
                    pe.wait_ge(kt_done, NTU * b + n - 1)
                for j in tr:
                    k = j - CHUNK * g
                    last = pe.transpose(ps_t[:, n % 2, k * P:(k + 1) * P],
                                        rows[:, place(j, par), i * P:(i + 1) * P], ident[:, :])
                last.then_inc(kt_ready, 1)

            def mix_batch(b, par, spread_before):
                n, half = 0, 0
                for g in range(G):
                    if g >= 2:
                        pe.wait_ge(y_out, G * b + g - 1)
                    started = [False, False]
                    for s, (i, nat, tr) in enumerate(mix[g]):
                        if g == 0 and s % CHUNK == 0:
                            pe.wait_ge(z_ready, G * b + G)
                        parts = []
                        if tr:
                            lo = tr[0] - CHUNK * g
                            if n + 2 < NTU:
                                turn_k(b, par, n + 2)
                            parts.append((lo, len(tr), kt[:, n % 3, lo * P:(lo + len(tr)) * P], n))
                            n += 1
                        if nat:
                            lo = nat[0] - CHUNK * g
                            parts.append((lo, len(nat), rows[:, place(i, par), nat[0] * P:(nat[-1] + 1) * P], None))
                        for lo, k, moving, item in parts:
                            if item is not None:
                                pe.wait_ge(kt_done, NTU * b + item + 1)
                            assert started[half] or k == CHUNK
                            last = pe.matmul(ps_a[C * half:C * half + C, g % 2, lo * P:(lo + k) * P], z[:, i, :], moving,
                                             start=not started[half], stop=True, skip_group_check=True)
                            started[half] = True
                            half = 1 - half
                            if item is not None:
                                last.then_inc(kt_used, 1)
                        if s == 1 and g >= 1:
                            turn_y(b, g - 1)
                        if s == 3 and g == 0 and spread_before:
                            spread_out(b - 1)
                    last.then_inc(y_ready, 1)

            def turn_y(b, g):
                pe.wait_ge(y_out, G * b + g + 1)
                if g == 0:
                    pe.wait_ge(scale_done, b + 1)
                else:
                    pe.wait_ge(n0_step, N0_STEPS * (G * b + g))
                for k in range(CHUNK):
                    last = pe.transpose(ps_v[:, k * P:(k + 1) * P], yt[:, g % 2, k * P:(k + 1) * P], ident[:, :])
                last.then_inc(y_turned, 1)

            def piece(b, t, par, n):
                m, h = pieces[n]
                if n == 0 and not (isinstance(b, int) and b == 0):
                    pe.wait_ge(n1_read, 2 * b)
                if h == 0:
                    pe.wait_ge(x1_ready, G * b + m // CHUNK + 1)
                    pe.wait_ge(adj_in[place(m, par)], loads(m, b, t, 2))
                for q in range(2):
                    g = 2 * h + q
                    last = pe.matmul(ps_o[C * q:C * q + C, h, :], xs[:, par, m, :],
                                     rows[:, place(m, par), g * CW:(g + 1) * CW],
                                     start=(m == spread_order[0]), stop=(m == spread_order[-1]), skip_group_check=True)
                if h == G // 2 - 1:
                    last.then_inc(row_used, 1)

            def spread_out(b):
                pe.wait_ge(u_out, 2 * b + 2)
                for h in range(G // 2):
                    for k in range(CHUNK):
                        for q in range(2):
                            o = (h * CHUNK + k) * C
                            last = pe.matmul(ps_o[:, q, o:o + C], ut[C * q:C * q + C, h, k * P:(k + 1) * P],
                                             weight2[C * q:C * q + C, :], start=True, stop=True, skip_group_check=True)
                last.then_inc(f_ready, 1)

            plan, planned = window_plan(T, chunks, NP)

            def window(b, t, par):
                for what, n in plan:
                    if what == "piece":
                        piece(b, t, par, n)
                    elif what == "turn":
                        turn_y(b, G - 1)
                    else:
                        j = chunks[n][0]
                        build_chunk(b + 1, t + par, 1 - par, n)
                        if first_of_row[j] == n and j >= 2:
                            column_sums(b + 1, 1 - par, j - 1)
                close_build(b + 1, 1 - par, [lambda n=n: piece(b, t, par, n) for n in range(planned, NP)])

            def close_build(b, par, rest):
                half = len(rest) // 2
                for f in rest[:half]:
                    f()
                column_sums(b, par, T - 1)
                turn_k(b, par, 0)
                turn_k(b, par, 1)
                for f in rest[half:]:
                    f()
                turn_sums(b)

            pe.wait_ge(u_split, 6 + 2 * len(PARTS) + 1)
            pe.wait_ge(const_set, 5)
            for e, ps in enumerate((ps_a, ps_t)):
                target = ps[:, :, :].rearrange("p b n -> p (b n)").bitcast(BF16)
                for tt in range(T):
                    last = pe.transpose(target[:, tt * P:(tt + 1) * P],
                                        u_stack[:, e, tt].rearrange("p s r -> p (s r)"), ident_b[:, :])
                last.then_inc(u_turned, 1)
            pe.wait_ge(u_ready, 2)
            pe.wait_ge(ident_1, 1)
            pe.wait_ge(const_in, 64)
            for c in range(NCH):
                build_chunk(0, 0, 0, c)
                j = chunks[c][0]
                if first_of_row[j] == c and j >= 2:
                    column_sums(0, 0, j - 1)
            close_build(0, 0, [])
            mix_batch(0, 0, False)
            window(0, 0, 0)
            with pe.Fori(0, B // 2 - 1) as t:
                mix_batch(2 * t + 1, 1, True)
                window(2 * t + 1, t, 1)
                mix_batch(2 * t + 2, 0, True)
                window(2 * t + 2, t + 1, 0)
            mix_batch(B - 1, 1, True)
            for n in range(NP):
                if n == 2:
                    turn_y(B - 1, G - 1)
                piece(B - 1, B // 2 - 1, 1, n)
            spread_out(B - 1)

        @block.scalar
        def _(act):
            def gates(b):
                for c, (j, g, blocks) in enumerate(chunks):
                    w = P * len(blocks)
                    act.wait_ge(gate_ready, NCH * b + c + 1)
                    if c >= 2 or not (isinstance(b, int) and b == 0):
                        act.wait_ge(k_done, NCH * b + c - 1)
                    act.activation(gate[:, c % 2, 0:w], ps_a[:, c % 2, 0:w], ACT.Sigmoid).then_inc(gate_done, 1)

            def degrees(b):
                act.activation(one[:, 1:2], one[:, 0:1], ACT.Sqrt)
                act.wait_ge(col_ready, b + 1)
                act.copy(sums[0:96, :], ps_c[0:96, :]).then_inc(col_out, 1)
                act.copy(sums[96:P, 0:CW - P], ps_c[96:P, 0:CW - P]).then_inc(col_out, 1)
                act.wait_ge(deg_step, DEG_STEPS * b + 3)
                act.activation(deg_root[:, :], deg[:, :], ACT.Sqrt).then_inc(root_done, 1)

            def spread_out(b):
                act.wait_ge(row_used, T * b + T)
                for h in range(G // 2):
                    act.copy(ut[:, h, :], ps_o[:, h, :]).then_inc(u_out, 1)

            def root_n0(b, g):
                act.wait_ge(n0_step, N0_STEPS * (G * b + g) + 10)
                act.activation(n0_root[:, g % 2, :], n0_var[:, g % 2, :], ACT.Sqrt).then_inc(n0_rooted, 1)

            def root_n1(b):
                act.wait_ge(n1_step, N1_STEPS * 2 * b + 16)
                for q in range(2):
                    act.activation(n1_root[:, q], n1_var[:, q], ACT.Sqrt).then_inc(n1_rooted, 1)

            def mix_batch(b, spread_before):
                firsts = [min(n for n, (g, _, _) in enumerate(turned) if g == gg) for gg in range(G)]

                def turn(n):
                    g, i, tr = turned[n]
                    lo, w = (tr[0] - CHUNK * g) * P, len(tr) * P
                    act.wait_ge(kt_ready, NTU * b + n + 1)
                    if n >= 3:
                        act.wait_ge(kt_used, NTU * b + n - 2)
                    act.copy(kt[:, n % 3, lo:lo + w], ps_t[:, n % 2, lo:lo + w]).then_inc(kt_done, 1)

                def leave(g):
                    act.wait_ge(y_ready, G * b + g + 1)
                    act.copy(yt[:, g % 2, :], ps_a[:, g % 2, :]).then_inc(y_out, 1)

                for n in range(NTU):
                    turn(n)
                    for g in range(1, G):
                        if n == firsts[g] + 1:
                            leave(g - 1)
                            if g == 2:
                                if spread_before:
                                    root_n1(b - 1)
                                root_n0(b, 0)
                            if g == 3:
                                root_n0(b, 1)
                leave(G - 1)
                root_n0(b, G - 2)
                root_n0(b, G - 1)

            act.wait_ge(const_set, 5)
            gates(0)
            degrees(0)
            mix_batch(0, False)
            gates(1)
            degrees(1)
            spread_out(0)
            with act.Fori(0, B // 2 - 1) as t:
                mix_batch(2 * t + 1, True)
                gates(2 * t + 2)
                degrees(2 * t + 2)
                spread_out(2 * t + 1)
                mix_batch(2 * t + 2, True)
                gates(2 * t + 3)
                degrees(2 * t + 3)
                spread_out(2 * t + 2)
            mix_batch(B - 1, True)
            spread_out(B - 1)
            act.wait_ge(n1_step, N1_STEPS * 2 * (B - 1) + 16)
            for q in range(2):
                act.activation(n1_root[:, q], n1_var[:, q], ACT.Sqrt).then_inc(n1_rooted, 1)

        @block.vector
        def _(dve):
            def build(b, par):
                def add(c):
                    j, g, blocks = chunks[c]
                    w = P * len(blocks)
                    k = rows[:, place(j, par), g * CW:g * CW + w]
                    dve.wait_ge(flip_ready, NCH * b + c + 1)
                    dve.tensor_tensor(k, k, ps_t[:, c % 2, 0:w], ALU.add).then_inc(sum_done, 1)

                def multiply(c):
                    j, g, blocks = chunks[c]
                    w = P * len(blocks)
                    k = rows[:, place(j, par), g * CW:g * CW + w]
                    dve.wait_ge(gate_done, NCH * b + c + 1)
                    dve.wait_ge(sum_done, NCH * b + c + 1)
                    dve.scalar_tensor_tensor(k, k, 1.0, gate[:, c % 2, 0:w], ALU.mult, ALU.mult,
                                             accum_out=row_sums[:, j, g:g + 1]).then_inc(k_done, 1)

                add(0)
                for c in range(NCH):
                    if c + 1 < NCH:
                        add(c + 1)
                    multiply(c)

            def degrees(b, t, par):
                base = DEG_STEPS * b
                dve.wait_ge(k_done, NCH * b + NCH)
                dve.tensor_reduce(row_sum[:, :], row_sums[:, :, :], AX_X, ALU.add).then_inc(deg_step, 1)
                dve.wait_ge(deg_step, base + 1)
                dve.wait_ge(col_turned, b + 1)
                col = ps_v[:, :].rearrange("p (k g r) -> p g k r", k=CHUNK, r=32)[:, :, :, 0]
                dve.tensor_tensor(deg[:, :].rearrange("p (g k) -> p g k", k=CHUNK),
                                  row_sum[:, :].rearrange("p (g k) -> p g k", k=CHUNK), col, ALU.add).then_inc(deg_step, 1)
                dve.wait_ge(deg_step, base + 2)
                dve.tensor_scalar(deg[:, :], deg[:, :], 0.5, DEG_EPS, ALU.mult, ALU.max).then_inc(deg_step, 1)
                dve.wait_ge(root_done, b + 1)
                dve.reciprocal(d[:, :], deg_root[:, :]).then_inc(deg_step, 1)
                dve.wait_ge(deg_step, base + 4)
                dve.wait_ge(x_in[par], 16 * t + 16)
                for g in range(G):
                    s = slice(CHUNK * g, CHUNK * g + CHUNK)
                    dve.tensor_tensor(z[:, s, :], xs[:, par, s, :],
                                      d[:, s].unsqueeze(2).to_broadcast([P, CHUNK, C]), ALU.mult).then_inc(z_ready, 1)
                dve.tensor_scalar(d_out[:, :], d[:, :], scale_b[:, 0:1], 0.5, ALU.mult, ALU.mult).then_inc(scale_done, 1)
                dve.wait_ge(scale_done, b + 1)

            def norm0_a(b, par, g):
                base = N0_STEPS * (G * b + g)
                step = [0]

                def link(ins):
                    step[0] += 1
                    ins.then_inc(n0_step, 1)
                    dve.wait_ge(n0_step, base + step[0])

                s = slice(CHUNK * g, CHUNK * g + CHUNK)
                xv = xs[:, par, s, :]
                y = ps_v[:, :].rearrange("p (k h c) -> p k h c", k=CHUNK, h=2)
                dv = d_out[:, s].unsqueeze(2).to_broadcast([P, CHUNK, C])
                sq = square[:, 0:CHUNK * C].rearrange("p (k c) -> p k c", c=C)
                dve.wait_ge(y_turned, G * b + g + 1)
                link(dve.tensor_tensor(part_a[:, :, :], y[:, :, 0, :], dv, ALU.mult))
                link(dve.tensor_tensor(part_b[:, :, :], y[:, :, 1, :], dv, ALU.mult))
                link(dve.tensor_tensor(part_a[:, :, :], part_a[:, :, :], part_b[:, :, :], ALU.add))
                link(dve.tensor_tensor(xv, xv, part_a[:, :, :], ALU.add))
                link(dve.tensor_reduce(n0_mean[:, :], xv, AX_X, ALU.add))
                link(dve.tensor_scalar(n0_mean[:, :], n0_mean[:, :], 1.0 / C, None, ALU.mult))
                link(dve.tensor_tensor(xv, xv, n0_mean[:, :].unsqueeze(2).to_broadcast([P, CHUNK, C]), ALU.subtract))
                link(dve.tensor_tensor(sq, xv, xv, ALU.mult))
                link(dve.tensor_reduce(n0_var[:, g % 2, :], sq, AX_X, ALU.add))
                link(dve.tensor_scalar(n0_var[:, g % 2, :], n0_var[:, g % 2, :], 1.0 / C, LN_EPS, ALU.mult, ALU.add))

            def norm0_b(b, par, g):
                s = slice(CHUNK * g, CHUNK * g + CHUNK)
                xv = xs[:, par, s, :]
                dve.wait_ge(n0_rooted, G * b + g + 1)
                dve.reciprocal(n0_inv[:, :], n0_root[:, g % 2, :]).then_inc(n0_step, 1)
                dve.wait_ge(n0_step, N0_STEPS * (G * b + g + 1))
                dve.tensor_tensor(xv, xv, n0_inv[:, :].unsqueeze(2).to_broadcast([P, CHUNK, C]),
                                  ALU.mult).then_inc(x1_ready, 1)
                dve.wait_ge(x1_ready, G * b + g + 1)

            def tiles(par, q):
                return xs[:, par].rearrange("p (h q k) c -> p q h k c", q=2, k=CHUNK)[:, q]

            def norm1_a(b, par, q):
                base = N1_STEPS * 2 * b + 8 * q
                step = [0]

                def link(ins):
                    step[0] += 1
                    ins.then_inc(n1_step, 1)
                    dve.wait_ge(n1_step, base + step[0])

                xv = tiles(par, q)
                sq = square[:, :].rearrange("p (h k c) -> p h k c", k=CHUNK, c=C)
                f = ps_o[:, q, :].rearrange("p (h k c) -> p h k c", k=CHUNK, c=C)
                dve.wait_ge(f_ready, b + 1)
                dve.tensor_tensor(xv, xv, f, ALU.add).then_inc(n1_read, 1)
                dve.wait_ge(n1_read, 2 * b + q + 1)
                for h in range(G // 2):
                    ins = dve.tensor_tensor(xv[:, h], xv[:, h], bias_b[:, :, :].to_broadcast([P, CHUNK, C]), ALU.add)
                    if h == 0:
                        ins.then_inc(n1_step, 1)
                step[0] = 1
                link(ins)
                link(dve.tensor_reduce(n1_mean[:, :, :], xv, AX_X, ALU.add))
                link(dve.tensor_scalar(n1_mean[:, :, :], n1_mean[:, :, :], 1.0 / C, None, ALU.mult))
                link(dve.tensor_tensor(xv, xv, n1_mean[:, :, :].unsqueeze(3).to_broadcast([P, G // 2, CHUNK, C]), ALU.subtract))
                link(dve.tensor_tensor(sq, xv, xv, ALU.mult))
                link(dve.tensor_reduce(n1_var[:, q], sq, AX_X, ALU.add))
                link(dve.tensor_scalar(n1_var[:, q], n1_var[:, q], 1.0 / C, LN_EPS, ALU.mult, ALU.add))
                assert step[0] == 8

            def norm1_b(b, par):
                for q in range(2):
                    xv = tiles(par, q)
                    dve.wait_ge(n1_rooted, 2 * b + q + 1)
                    dve.reciprocal(n1_inv[:, :, :], n1_root[:, q]).then_inc(n1_step, 1)
                    dve.wait_ge(n1_step, N1_STEPS * 2 * b + 17 + q)
                    dve.tensor_tensor(xv, xv, n1_inv[:, :, :].unsqueeze(3).to_broadcast([P, G // 2, CHUNK, C]),
                                      ALU.mult).then_inc(out_ready, 1)
                    dve.wait_ge(out_ready, 2 * b + q + 1)

            def mix_batch(b, par, spread_before):
                if spread_before:
                    norm1_a(b - 1, 1 - par, 0)
                    norm1_a(b - 1, 1 - par, 1)
                norm0_a(b, par, 0)
                if spread_before:
                    norm1_b(b - 1, 1 - par)
                norm0_b(b, par, 0)
                for g in range(1, G):
                    norm0_a(b, par, g)
                    norm0_b(b, par, g)

            dve.memset(ones[:, :], 1.0).then_inc(const_set, 1)
            dve.memset(row_sums[:, :, :], 0.0).then_inc(const_set, 1)
            dve.memset(sums[96:P, CW - P:CW], 0.0).then_inc(const_set, 1)
            dve.memset(one[:, 0:1], 1.0).then_inc(const_set, 1)
            dve.wait_ge(ident_1, 1)
            dve.tensor_copy(ident_b[:, :], ident[:, :]).then_inc(const_set, 1)
            dve.wait_ge(const_set, 5)
            split = [0]

            def link(ins):
                split[0] += 1
                ins.then_inc(u_split, 1)
                dve.wait_ge(u_split, split[0])

            dve.wait_ge(u_in_done, 16)
            link(dve.tensor_copy(u_part[:, 0], u_in))
            link(dve.tensor_tensor(u_rest, u_in, u_part[:, 0], ALU.subtract))
            link(dve.tensor_copy(u_part[:, 1], u_rest))
            link(dve.tensor_tensor(u_rest2, u_rest, u_part[:, 1], ALU.subtract))
            link(dve.tensor_copy(u_part[:, 2], u_rest2))
            for e in range(2):
                for s, pair in enumerate(PARTS):
                    link(dve.tensor_copy(u_stack[:, e, :, s, :], u_part[:, pair[e]]))
            link(dve.memset(one[:, 0:1], 1.0))
            link(dve.memset(one[:, 0:1], 1.0))
            for e, (ps, to) in enumerate(((ps_a, u_left), (ps_t, u_right))):
                dve.wait_ge(u_turned, e + 1)
                dve.tensor_copy(to[:, :], ps[:, :, :].rearrange("p b n -> p (b n)").bitcast(BF16)).then_inc(u_ready, 1)
            dve.wait_ge(u_ready, 2)
            dve.wait_ge(const_in, 64)

            build(0, 0)
            degrees(0, 0, 0)
            mix_batch(0, 0, False)
            build(1, 1)
            degrees(1, 0, 1)
            with dve.Fori(0, B // 2 - 1) as t:
                mix_batch(2 * t + 1, 1, True)
                build(2 * t + 2, 0)
                degrees(2 * t + 2, t + 1, 0)
                mix_batch(2 * t + 2, 0, True)
                build(2 * t + 3, 1)
                degrees(2 * t + 3, t + 1, 1)
            mix_batch(B - 1, 1, True)
            norm1_a(B - 1, 1, 0)
            norm1_a(B - 1, 1, 1)
            norm1_b(B - 1, 1)


_INS = ["x", "adj", "L0_gnn_U", "L0_gnn_w_scale", "L1_gnn_weight", "L1_gnn_bias"]


def kernel(**inputs):
    import numpy as _np
    import concourse.bacc as _bacc
    from concourse import mybir as _mybir
    from concourse.bass_utils import run_bass_kernel_spmd as _run

    nc = _bacc.Bacc("TRN2", target_bir_lowering=False, num_devices=1)
    arrays, args = {}, []
    for name in _INS:
        a = _np.ascontiguousarray(inputs[name])
        if a.ndim == 0:
            a = a.reshape(1)
        arrays[f"in_{name}"] = a
        args.append(nc.dram_tensor(f"in_{name}", a.shape, _mybir.dt.from_np(a.dtype), kind="ExternalInput").ap())
    out = nc.dram_tensor("out", inputs["x"].shape, F32, kind="ExternalOutput").ap()
    graph_layers(nc, *args, out)
    r = _run(nc, [arrays], core_ids=[0])
    return r.results[0]["out"]
```

```python
from contextlib import ExitStack

import concourse.bass as bass
from concourse import mybir

F32 = mybir.dt.float32
BF16 = mybir.dt.bfloat16
ALU = mybir.AluOpType
ACT = mybir.ActivationFunctionType
AX_X = mybir.AxisListType.X

P = 128
CHUNK = 4
CW = CHUNK * P
DEG_EPS = 1e-12
LN_EPS = 1e-5
PARTS = ((0, 0), (0, 1), (1, 0), (1, 1), (0, 2), (2, 0), (1, 2), (2, 1))
EARLY = 4
UPFRONT = 14
HALFWAY = 24
SOON = 20
TAIL = 4

DEG_STEPS = 4
N0_STEPS = 11
N1_STEPS = 8


def build_chunks(T):
    return [(j, g, list(range(CHUNK * g, min(CHUNK * g + CHUNK, j + 1)))) for j in range(T) for g in range(j // CHUNK + 1)]


def mix_steps(T):
    out = []
    for g in range(T // CHUNK):
        blocks = range(CHUNK * g, CHUNK * g + CHUNK)
        rows = [(i, [j for j in blocks if j <= i], [j for j in blocks if j > i]) for i in range(T)]
        rows.sort(key=lambda r: 0 if not r[2] else 1 if not r[1] else 2)
        out.append(rows)
    return out


def window_plan(T, chunks, pieces):
    early = [c for c, (j, _, _) in enumerate(chunks) if j < EARLY]
    late = [c for c, (j, _, _) in enumerate(chunks) if j >= EARLY]
    plan = [("piece", 0), ("piece", 1), ("turn", 0)] + [("piece", n) for n in range(2, 8)]
    n = 8
    for c in early:
        plan += [("chunk", c), ("piece", n)]
        n += 1
    upfront, tail = UPFRONT, TAIL
    while n < upfront:
        plan.append(("piece", n))
        n += 1
    for k, c in enumerate(late):
        plan.append(("chunk", c))
        while n < (upfront + (k + 1) * (HALFWAY - upfront) // SOON if k < SOON else
                   HALFWAY + (k + 1 - SOON) * (pieces - HALFWAY - tail) // (len(late) - SOON)):
            plan.append(("piece", n))
            n += 1
    return plan, n


def graph_layers(nc, x, adj, u, w_scale, weight, bias, out):
    B, N, C = x.shape
    R = u.shape[1]
    T = N // P
    G = T // CHUNK
    chunks = build_chunks(T)
    NCH = len(chunks)
    mix = mix_steps(T)
    turned = [(g, i, tr) for g in range(G) for i, _, tr in mix[g] if tr]
    NTU = len(turned)
    spread_order = list(range(EARLY, T)) + list(range(EARLY))
    pieces = [(m, h) for m in spread_order for h in range(G // 2)]
    NP = len(pieces)
    ONES_FROM = T - 2
    SUMMED = sum(1 for j, g, _ in chunks if 0 < j < ONES_FROM and CHUNK * g < j)
    first_of_row = {}
    for c, (j, _, _) in enumerate(chunks):
        first_of_row.setdefault(j, c)

    adj_rows = adj.rearrange("b (r p) n -> b r p n", p=P)
    x_tiles = x.rearrange("b (t p) c -> b p t c", p=P)
    out_tiles = out.rearrange("b (t p) c -> b p t c", p=P)

    def place(row, par):
        return row if row >= EARLY or par == 0 else T + row

    def loads(row, b, t, n):
        again = G if row >= T - CHUNK else 1
        return 16 * ((1 + again) * (b if row >= EARLY else t) + (1 if n == 1 else 1 + again))

    with ExitStack() as ctx:
        def sb(name, shape, dt=F32):
            return ctx.enter_context(nc.sbuf_tensor(name, shape, dt))

        def pb(name, shape, dt=F32):
            return ctx.enter_context(nc.psum_tensor(name, shape, dt))

        def sem(name):
            return ctx.enter_context(nc.semaphore(name))

        rows = sb("rows", [P, T + EARLY, N])
        xs = sb("xs", [P, 2, T, C])
        shared = sb("shared", [P, N])
        z = shared[:, 0:T * C].rearrange("p (t c) -> p t c", c=C)
        u_left = sb("u_left", [P, N], BF16)
        u_right = sb("u_right", [P, N], BF16)
        gate = sb("gate", [P, 2, CW])
        kt_last = sb("kt_last", [P, CW])
        kt = [shared[:, T * C:T * C + CW], shared[:, T * C + CW:T * C + 2 * CW], kt_last[:, :]]
        yt = sb("yt", [P, 2, CW])
        ut = sb("ut", [P, G // 2, CW])
        sums = sb("sums", [P, CW])
        square = sb("square", [P, T, C])
        part_a = square[:, CHUNK:2 * CHUNK]
        part_b = square[:, 2 * CHUNK:3 * CHUNK]
        ident = sb("ident", [P, P])
        ident_b = sb("ident_b", [P, P], BF16)
        ones = sb("ones", [P, 32])
        weight2 = sb("weight2", [P, C])
        bias_b = sb("bias_b", [P, 1, C])
        scale_b = sb("scale_b", [P, 1])
        row_sums = sb("row_sums", [P, T, G])
        row_sum = sb("row_sum", [P, T])
        deg = sb("deg", [P, T])
        deg_root = sb("deg_root", [P, T])
        d = sb("d", [P, T])
        d_out = sb("d_out", [P, T])
        n0_mean = sb("n0_mean", [P, CHUNK])
        n0_var = sb("n0_var", [P, 2, CHUNK])
        n0_root = sb("n0_root", [P, 2, CHUNK])
        n0_inv = sb("n0_inv", [P, CHUNK])
        n1_mean = sb("n1_mean", [P, T])
        n1_var = sb("n1_var", [P, T])
        n1_root = sb("n1_root", [P, T])
        n1_inv = sb("n1_inv", [P, T])
        one = sb("one", [P, 2])
        zero = sb("zero", [P, 1])

        ps_a = pb("ps_a", [P, 2, CW])
        ps_t = pb("ps_t", [P, 2, CW])
        ps_o = pb("ps_o", [P, 2, CW])
        ps_c = pb("ps_c", [P, CW])
        ps_v = pb("ps_v", [P, CW])

        u_in = rows[:, T + 2, 0:T * R].rearrange("p (t r) -> p t r", r=R)
        u_rest = rows[:, T + 2, 512:512 + T * R].rearrange("p (t r) -> p t r", r=R)
        u_rest2 = rows[:, T + 2, 1024:1024 + T * R].rearrange("p (t r) -> p t r", r=R)
        u_part = rows[:, T + 2, 1536:1536 + 3 * T * R // 2].bitcast(BF16).rearrange("p (s t r) -> p s t r", s=3, r=R)
        u_stack = rows[:, T + 3, :].bitcast(BF16).rearrange("p (e t s r) -> p e t s r", e=2, t=T, r=R)

        adj_in = [sem(f"adj_in{r}") for r in range(T + EARLY)]
        x_in = [sem("x_in0"), sem("x_in1")]
        u_in_done = sem("u_in_done")
        const_in = sem("const_in")
        ident_0 = sem("ident_0")
        ident_1 = sem("ident_1")
        const_set = sem("const_set")
        u_split = sem("u_split")
        u_turned = sem("u_turned")
        u_ready = sem("u_ready")
        gate_ready = sem("gate_ready")
        gate_done = sem("gate_done")
        flip_ready = sem("flip_ready")
        sum_done = sem("sum_done")
        acc_step = sem("acc_step")
        sums_zero = sem("sums_zero")
        k_done = sem("k_done")
        col_ready = sem("col_ready")
        col_out = sem("col_out")
        col_turned = sem("col_turned")
        deg_step = sem("deg_step")
        root_done = sem("root_done")
        z_ready = sem("z_ready")
        scale_done = sem("scale_done")
        kt_ready = sem("kt_ready")
        kt_done = sem("kt_done")
        kt_used = sem("kt_used")
        y_ready = sem("y_ready")
        y_out = sem("y_out")
        y_turned = sem("y_turned")
        n0_step = sem("n0_step")
        n0_rooted = sem("n0_rooted")
        x1_ready = sem("x1_ready")
        row_used = sem("row_used")
        u_out = sem("u_out")
        f_ready = sem("f_ready")
        n1_step = sem("n1_step")
        n1_rooted = sem("n1_rooted")
        n1_read = sem("n1_read")
        out_ready = sem("out_ready")
        stored = sem("stored")

        block = ctx.enter_context(nc.Block())

        @block.sync
        def _(sp):
            def load_row(b, t, par, row):
                sp.dma_start(rows[:, place(row, par), :], adj_rows[b, row]).then_inc(adj_in[place(row, par)], 16)

            def store(b, par):
                sp.wait_ge(out_ready, b + 1)
                sp.dma_start(out_tiles[b], xs[:, par]).then_inc(stored, 16)

            def behind_the_mix(b, t, par, spread_before=True, last=False):
                if not last:
                    if spread_before:
                        sp.wait_ge(row_used, T * b)
                    else:
                        sp.wait_ge(u_ready, 2)
                    for row in range(EARLY):
                        load_row(b + 1, t + par, 1 - par, row)
                for g in range(G):
                    sp.wait_ge(y_ready, G * b + g + 1)
                    if g == 2 and spread_before:
                        store(b - 1, 1 - par)
                    if g < G - 1:
                        for row in range(CHUNK * g, CHUNK * g + CHUNK):
                            load_again(b, par, row, 0, row + 1)
                    if g == G - 2:
                        for h in range(G - 1):
                            sp.wait_ge(kt_ready, NTU * b + NTU - T + 1 + CHUNK * (h + 1))
                            for row in range(CHUNK * (G - 1), T):
                                load_again(b, par, row, CHUNK * h, CHUNK * (h + 1))
                    if g == G - 1:
                        for row in range(CHUNK * (G - 1), T):
                            load_again(b, par, row, CHUNK * (G - 1), row + 1)
                    if g == G - 1 and not last:
                        if spread_before:
                            sp.wait_ge(stored, 16 * b)
                        sp.dma_start(xs[:, 1 - par], x_tiles[b + 1]).then_inc(x_in[1 - par], 16)

            def load_again(b, par, row, lo, hi):
                sp.dma_start(rows[:, place(row, par), lo * P:hi * P], adj_rows[b, row][:, lo * P:hi * P]).then_inc(
                    adj_in[place(row, par)], 16)

            def behind_the_spread(b, t, par):
                for n, row in enumerate(spread_order[:T - EARLY]):
                    sp.wait_ge(row_used, T * b + n + 1)
                    load_row(b + 1, t + par, 1 - par, row)

            for row in range(T):
                load_row(0, 0, 0, row)
            sp.dma_start(xs[:, 0], x_tiles[0]).then_inc(x_in[0], 16)
            behind_the_mix(0, 0, 0, spread_before=False)
            behind_the_spread(0, 0, 0)
            with sp.Fori(0, B // 2 - 1) as t:
                behind_the_mix(2 * t + 1, t, 1)
                behind_the_spread(2 * t + 1, t, 1)
                behind_the_mix(2 * t + 2, t + 1, 0)
                behind_the_spread(2 * t + 2, t + 1, 0)
            behind_the_mix(B - 1, B // 2 - 1, 1, last=True)
            store(B - 1, 1)
            sp.wait_ge(stored, 16 * B)

        @block.gpsimd
        def _(pool):
            pool.memset(ident[:, :], 0.0).then_inc(ident_0, 1)
            pool.wait_ge(ident_0, 1)
            pool.affine_select(out=ident[:, :], in_=ident[:, :], compare_op=ALU.not_equal, fill=1.0, base=0,
                               pattern=[[-1, P]], channel_multiplier=1).then_inc(ident_1, 1)

            def column_sums(b, par):
                base = SUMMED * b
                pool.wait_ge(sums_zero, b + 1)
                n = 0
                for c, (j, g, blocks) in enumerate(chunks):
                    w = P * len([i for i in blocks if i < j])
                    if j >= ONES_FROM or not w:
                        continue
                    pool.wait_ge(k_done, NCH * b + c + 1)
                    if n:
                        pool.wait_ge(acc_step, base + n)
                    acc = shared[:, g * CW:g * CW + w]
                    pool.tensor_tensor(acc, acc, rows[:, place(j, par), g * CW:g * CW + w], ALU.add).then_inc(acc_step, 1)
                    n += 1

            column_sums(0, 0)
            column_sums(1, 1)
            with pool.Fori(0, B // 2 - 1) as t:
                column_sums(2 * t + 2, 0)
                column_sums(2 * t + 3, 1)

        @block.tensor
        def _(pe):
            def build_chunk(b, t, par, c):
                j, g, blocks = chunks[c]
                w = P * len(blocks)
                buf = c % 2
                if c < 2:
                    if not (isinstance(b, int) and b == 0):
                        pe.wait_ge(y_out, G * b)
                else:
                    pe.wait_ge(gate_done, NCH * b + c - 1)
                pe.matmul(ps_a[:, buf, 0:w], u_left[:, j * P:(j + 1) * P], u_right[:, g * CW:g * CW + w],
                          start=True, stop=True).then_inc(gate_ready, 1)
                if first_of_row[j] == c:
                    pe.wait_ge(adj_in[place(j, par)], loads(j, b, t, 1))
                if c >= 2:
                    pe.wait_ge(sum_done, NCH * b + c - 1)
                for k, i in enumerate(blocks):
                    last = pe.transpose(ps_t[:, buf, k * P:(k + 1) * P],
                                        rows[:, place(i, par), j * P:(j + 1) * P], ident[:, :])
                last.then_inc(flip_ready, 1)

            def column_sums(b, par, j):
                if j == ONES_FROM:
                    pe.wait_ge(acc_step, SUMMED * (b + 1))
                    for g in range(G):
                        pe.matmul(ps_c[32 * g:32 * g + 32, :], ones[:, :], shared[:, g * CW:(g + 1) * CW],
                                  start=True, stop=False, skip_group_check=True)
                for g in range(G):
                    w = min(CW, (j - CHUNK * g) * P)
                    pe.wait_ge(k_done, NCH * b + first_of_row[j] + g + 1)
                    last = pe.matmul(ps_c[32 * g:32 * g + 32, 0:w], ones[:, :],
                                     rows[:, place(j, par), g * CW:g * CW + w],
                                     start=False, stop=(j == T - 1), skip_group_check=True)
                if j == T - 1:
                    last.then_inc(col_ready, 1)

            def turn_sums(b):
                pe.wait_ge(col_out, b + 1)
                if not (isinstance(b, int) and b == 0):
                    pe.wait_ge(n0_step, N0_STEPS * G * b)
                for k in range(CHUNK):
                    last = pe.transpose(ps_v[:, k * P:(k + 1) * P], sums[:, k * P:(k + 1) * P], ident[:, :])
                last.then_inc(col_turned, 1)

            def turn_k(b, par, n):
                g, i, tr = turned[n]
                if n < 2:
                    pe.wait_ge(k_done, NCH * b + NCH)
                else:
                    pe.wait_ge(kt_done, NTU * b + n - 1)
                for j in tr:
                    k = j - CHUNK * g
                    last = pe.transpose(ps_t[:, n % 2, k * P:(k + 1) * P],
                                        rows[:, place(j, par), i * P:(i + 1) * P], ident[:, :])
                last.then_inc(kt_ready, 1)

            def mix_batch(b, par, spread_before):
                n, half = 0, 0
                for g in range(G):
                    if g >= 2:
                        pe.wait_ge(y_out, G * b + g - 1)
                    started = [False, False]
                    for s, (i, nat, tr) in enumerate(mix[g]):
                        if g == 0:
                            pe.wait_ge(z_ready, G * b + i // CHUNK + 1)
                        parts = []
                        if tr:
                            lo = tr[0] - CHUNK * g
                            if n + 2 < NTU:
                                turn_k(b, par, n + 2)
                            parts.append((lo, len(tr), kt[n % 3][:, lo * P:(lo + len(tr)) * P], n))
                            n += 1
                        if nat:
                            lo = nat[0] - CHUNK * g
                            parts.append((lo, len(nat), rows[:, place(i, par), nat[0] * P:(nat[-1] + 1) * P], None))
                        for lo, k, moving, item in parts:
                            if item is not None:
                                pe.wait_ge(kt_done, NTU * b + item + 1)
                            assert started[half] or k == CHUNK
                            last = pe.matmul(ps_a[C * half:C * half + C, g % 2, lo * P:(lo + k) * P], z[:, i], moving,
                                             start=not started[half], stop=True, skip_group_check=True)
                            started[half] = True
                            half = 1 - half
                            if item is not None:
                                last.then_inc(kt_used, 1)
                        if s == 1 and g >= 1:
                            turn_y(b, g - 1)
                        if s == 3 and g == 0 and spread_before:
                            spread_out(b - 1)
                    last.then_inc(y_ready, 1)

            def turn_y(b, g):
                pe.wait_ge(y_out, G * b + g + 1)
                if g == 0:
                    pe.wait_ge(scale_done, b + 1)
                else:
                    pe.wait_ge(n0_step, N0_STEPS * (G * b + g))
                for k in range(CHUNK):
                    last = pe.transpose(ps_v[:, k * P:(k + 1) * P], yt[:, g % 2, k * P:(k + 1) * P], ident[:, :])
                last.then_inc(y_turned, 1)

            def piece(b, t, par, n):
                m, h = pieces[n]
                if n == 0 and not (isinstance(b, int) and b == 0):
                    pe.wait_ge(n1_read, 2 * b)
                if h == 0:
                    pe.wait_ge(x1_ready, G * b + m // CHUNK + 1)
                    pe.wait_ge(adj_in[place(m, par)], loads(m, b, t, 2))
                for q in range(2):
                    g = 2 * h + q
                    last = pe.matmul(ps_o[C * q:C * q + C, h, :], xs[:, par, m, :],
                                     rows[:, place(m, par), g * CW:(g + 1) * CW],
                                     start=(m == spread_order[0]), stop=(m == spread_order[-1]), skip_group_check=True)
                if h == G // 2 - 1:
                    last.then_inc(row_used, 1)

            def spread_out(b):
                pe.wait_ge(u_out, 2 * b + 2)
                pe.wait_ge(const_in, 64)
                for h in range(G // 2):
                    for k in range(CHUNK):
                        for q in range(2):
                            o = (h * CHUNK + k) * C
                            last = pe.matmul(ps_o[:, q, o:o + C], ut[C * q:C * q + C, h, k * P:(k + 1) * P],
                                             weight2[C * q:C * q + C, :], start=True, stop=True, skip_group_check=True)
                last.then_inc(f_ready, 1)

            plan, planned = window_plan(T, chunks, NP)

            def window(b, t, par):
                for what, n in plan:
                    if what == "piece":
                        piece(b, t, par, n)
                    elif what == "turn":
                        turn_y(b, G - 1)
                    else:
                        build_chunk(b + 1, t + par, 1 - par, n)
                close_build(b + 1, 1 - par, [lambda n=n: piece(b, t, par, n) for n in range(planned, NP)])

            def close_build(b, par, rest):
                for f in rest[:2]:
                    f()
                column_sums(b, par, T - 2)
                column_sums(b, par, T - 1)
                turn_k(b, par, 0)
                turn_k(b, par, 1)
                for f in rest[2:3]:
                    f()
                turn_sums(b)
                for f in rest[3:]:
                    f()

            pe.wait_ge(u_split, 6 + 2 * len(PARTS) + 1)
            pe.wait_ge(const_set, 5)
            for e, ps in enumerate((ps_a, ps_t)):
                target = ps[:, :, :].rearrange("p b n -> p (b n)").bitcast(BF16)
                for tt in range(T):
                    last = pe.transpose(target[:, tt * P:(tt + 1) * P],
                                        u_stack[:, e, tt].rearrange("p s r -> p (s r)"), ident_b[:, :])
                last.then_inc(u_turned, 1)
            pe.wait_ge(u_ready, 2)
            pe.wait_ge(ident_1, 1)
            for c in range(NCH):
                build_chunk(0, 0, 0, c)
            close_build(0, 0, [])
            mix_batch(0, 0, False)
            window(0, 0, 0)
            with pe.Fori(0, B // 2 - 1) as t:
                mix_batch(2 * t + 1, 1, True)
                window(2 * t + 1, t, 1)
                mix_batch(2 * t + 2, 0, True)
                window(2 * t + 2, t + 1, 0)
            mix_batch(B - 1, 1, True)
            for n in range(NP):
                if n == 2:
                    turn_y(B - 1, G - 1)
                piece(B - 1, B // 2 - 1, 1, n)
            spread_out(B - 1)

        @block.scalar
        def _(act):
            def gates(b):
                for c, (j, g, blocks) in enumerate(chunks):
                    w = P * len(blocks)
                    act.wait_ge(gate_ready, NCH * b + c + 1)
                    if c >= 2 or not (isinstance(b, int) and b == 0):
                        act.wait_ge(k_done, NCH * b + c - 1)
                    act.activation(gate[:, c % 2, 0:w], ps_a[:, c % 2, 0:w], ACT.Sigmoid).then_inc(gate_done, 1)

            def degrees(b):
                act.activation(one[:, 1:2], one[:, 0:1], ACT.Sqrt)
                act.wait_ge(col_ready, b + 1)
                act.copy(sums[:, :], ps_c[:, :]).then_inc(col_out, 1)
                act.wait_ge(deg_step, DEG_STEPS * b + 3)
                act.activation(deg_root[:, :], deg[:, :], ACT.Sqrt).then_inc(root_done, 1)

            def spread_out(b):
                act.wait_ge(row_used, T * b + T)
                for h in range(G // 2):
                    act.copy(ut[:, h, :], ps_o[:, h, :]).then_inc(u_out, 1)

            def root_n0(b, g):
                act.wait_ge(n0_step, N0_STEPS * (G * b + g) + 10)
                act.activation(n0_root[:, g % 2, :], n0_var[:, g % 2, :], ACT.Sqrt).then_inc(n0_rooted, 1)

            def root_n1(b):
                act.wait_ge(n1_step, N1_STEPS * b + 7)
                act.activation(n1_root[:, :], n1_var[:, :], ACT.Sqrt).then_inc(n1_rooted, 1)

            def mix_batch(b, spread_before):
                firsts = [min(n for n, (g, _, _) in enumerate(turned) if g == gg) for gg in range(G)]

                def turn(n):
                    g, i, tr = turned[n]
                    lo, w = (tr[0] - CHUNK * g) * P, len(tr) * P
                    act.wait_ge(kt_ready, NTU * b + n + 1)
                    if n >= 3:
                        act.wait_ge(kt_used, NTU * b + n - 2)
                    act.copy(kt[n % 3][:, lo:lo + w], ps_t[:, n % 2, lo:lo + w]).then_inc(kt_done, 1)

                def leave(g):
                    act.wait_ge(y_ready, G * b + g + 1)
                    act.copy(yt[:, g % 2, :], ps_a[:, g % 2, :]).then_inc(y_out, 1)

                for n in range(NTU):
                    turn(n)
                    for g in range(1, G):
                        if n == firsts[g] + 1:
                            leave(g - 1)
                    if n == firsts[1] + 5:
                        if spread_before:
                            root_n1(b - 1)
                        root_n0(b, 0)
                    if n == firsts[2] + 8:
                        root_n0(b, 1)
                    if n == firsts[3] + 9:
                        root_n0(b, 2)
                leave(G - 1)
                clear_sums()
                root_n0(b, G - 1)

            def clear_sums():
                act.copy(shared[:, :], zero[:, :].to_broadcast([P, N])).then_inc(sums_zero, 1)

            def build(b):
                gates(b)
                degrees(b)

            act.dma_start(u_in, u.rearrange("(t p) r -> p t r", p=P)).then_inc(u_in_done, 16)
            act.dma_start(weight2[0:C, :], weight).then_inc(const_in, 16)
            act.dma_start(weight2[C:2 * C, :], weight).then_inc(const_in, 16)
            act.dma_start(bias_b[:, 0, :], bias.partition_broadcast(P)).then_inc(const_in, 16)
            act.dma_start(scale_b[:, :], w_scale.partition_broadcast(P)).then_inc(const_in, 16)
            act.wait_ge(const_set, 5)
            clear_sums()
            build(0)
            mix_batch(0, False)
            build(1)
            spread_out(0)
            with act.Fori(0, B // 2 - 1) as t:
                mix_batch(2 * t + 1, True)
                build(2 * t + 2)
                spread_out(2 * t + 1)
                mix_batch(2 * t + 2, True)
                build(2 * t + 3)
                spread_out(2 * t + 2)
            mix_batch(B - 1, True)
            spread_out(B - 1)
            root_n1(B - 1)

        @block.vector
        def _(dve):
            def build(b, par):
                def add(c):
                    j, g, blocks = chunks[c]
                    w = P * len(blocks)
                    k = rows[:, place(j, par), g * CW:g * CW + w]
                    dve.wait_ge(flip_ready, NCH * b + c + 1)
                    dve.tensor_tensor(k, k, ps_t[:, c % 2, 0:w], ALU.add).then_inc(sum_done, 1)

                def multiply(c):
                    j, g, blocks = chunks[c]
                    w = P * len(blocks)
                    k = rows[:, place(j, par), g * CW:g * CW + w]
                    dve.wait_ge(gate_done, NCH * b + c + 1)
                    dve.wait_ge(sum_done, NCH * b + c + 1)
                    dve.scalar_tensor_tensor(k, k, 1.0, gate[:, c % 2, 0:w], ALU.mult, ALU.mult,
                                             accum_out=row_sums[:, j, g:g + 1]).then_inc(k_done, 1)

                for c in range(NCH):
                    if c == 0:
                        add(c)
                    if c + 1 < NCH:
                        add(c + 1)
                    multiply(c)

            def degrees(b, t, par):
                base = DEG_STEPS * b
                dve.wait_ge(k_done, NCH * b + NCH)
                dve.tensor_reduce(row_sum[:, :], row_sums[:, :, :], AX_X, ALU.add).then_inc(deg_step, 1)
                dve.wait_ge(deg_step, base + 1)
                dve.wait_ge(col_turned, b + 1)
                col = ps_v[:, :].rearrange("p (k g r) -> p g k r", k=CHUNK, r=32)[:, :, :, 0]
                dve.tensor_tensor(deg[:, :].rearrange("p (g k) -> p g k", k=CHUNK),
                                  row_sum[:, :].rearrange("p (g k) -> p g k", k=CHUNK), col, ALU.add).then_inc(deg_step, 1)
                dve.wait_ge(deg_step, base + 2)
                dve.tensor_scalar(deg[:, :], deg[:, :], 0.5, DEG_EPS, ALU.mult, ALU.max).then_inc(deg_step, 1)
                dve.wait_ge(root_done, b + 1)
                dve.reciprocal(d[:, :], deg_root[:, :]).then_inc(deg_step, 1)
                dve.wait_ge(deg_step, base + 4)
                dve.wait_ge(x_in[par], 16 * t + 16)
                for g in range(G):
                    s = slice(CHUNK * g, CHUNK * g + CHUNK)
                    dve.tensor_tensor(z[:, s, :], xs[:, par, s, :],
                                      d[:, s].unsqueeze(2).to_broadcast([P, CHUNK, C]), ALU.mult).then_inc(z_ready, 1)
                dve.wait_ge(const_in, 64)
                dve.tensor_scalar(d_out[:, :], d[:, :], scale_b[:, 0:1], 0.5, ALU.mult, ALU.mult).then_inc(scale_done, 1)
                dve.wait_ge(scale_done, b + 1)

            def norm0_a(b, par, g):
                base = N0_STEPS * (G * b + g)
                step = [0]

                def link(ins):
                    step[0] += 1
                    ins.then_inc(n0_step, 1)
                    dve.wait_ge(n0_step, base + step[0])

                s = slice(CHUNK * g, CHUNK * g + CHUNK)
                xv = xs[:, par, s, :]
                y = ps_v[:, :].rearrange("p (k h c) -> p k h c", k=CHUNK, h=2)
                dv = d_out[:, s].unsqueeze(2).to_broadcast([P, CHUNK, C])
                sq = square[:, 0:CHUNK]
                dve.wait_ge(y_turned, G * b + g + 1)
                link(dve.tensor_tensor(part_a, y[:, :, 0, :], dv, ALU.mult))
                link(dve.tensor_tensor(part_b, y[:, :, 1, :], dv, ALU.mult))
                link(dve.tensor_tensor(part_a, part_a, part_b, ALU.add))
                link(dve.tensor_tensor(xv, xv, part_a, ALU.add))
                link(dve.tensor_reduce(n0_mean[:, :], xv, AX_X, ALU.add))
                link(dve.tensor_scalar(n0_mean[:, :], n0_mean[:, :], 1.0 / C, None, ALU.mult))
                link(dve.tensor_tensor(xv, xv, n0_mean[:, :].unsqueeze(2).to_broadcast([P, CHUNK, C]), ALU.subtract))
                link(dve.tensor_tensor(sq, xv, xv, ALU.mult))
                link(dve.tensor_reduce(n0_var[:, g % 2, :], sq, AX_X, ALU.add))
                link(dve.tensor_scalar(n0_var[:, g % 2, :], n0_var[:, g % 2, :], 1.0 / C, LN_EPS, ALU.mult, ALU.add))

            def norm0_b(b, par, g):
                s = slice(CHUNK * g, CHUNK * g + CHUNK)
                xv = xs[:, par, s, :]
                dve.wait_ge(n0_rooted, G * b + g + 1)
                dve.reciprocal(n0_inv[:, :], n0_root[:, g % 2, :]).then_inc(n0_step, 1)
                dve.wait_ge(n0_step, N0_STEPS * (G * b + g + 1))
                dve.tensor_tensor(xv, xv, n0_inv[:, :].unsqueeze(2).to_broadcast([P, CHUNK, C]),
                                  ALU.mult).then_inc(x1_ready, 1)
                dve.wait_ge(x1_ready, G * b + g + 1)

            def norm1_first(b, par):
                dve.wait_ge(f_ready, b + 1)
                for q in range(2):
                    xv = xs[:, par].rearrange("p (h q k) c -> p q h k c", q=2, k=CHUNK)[:, q]
                    f = ps_o[:, q, :].rearrange("p (h k c) -> p h k c", k=CHUNK, c=C)
                    dve.tensor_tensor(xv, xv, f, ALU.add).then_inc(n1_read, 1)

            def norm1_a(b, par):
                step = [0]

                def link(ins):
                    step[0] += 1
                    ins.then_inc(n1_step, 1)
                    dve.wait_ge(n1_step, N1_STEPS * b + step[0])

                xv = xs[:, par]
                dve.wait_ge(n1_read, 2 * b + 2)
                link(dve.tensor_tensor(xv, xv, bias_b[:, :, :].to_broadcast([P, T, C]), ALU.add))
                link(dve.tensor_reduce(n1_mean[:, :], xv, AX_X, ALU.add))
                link(dve.tensor_scalar(n1_mean[:, :], n1_mean[:, :], 1.0 / C, None, ALU.mult))
                link(dve.tensor_tensor(xv, xv, n1_mean[:, :].unsqueeze(2).to_broadcast([P, T, C]), ALU.subtract))
                link(dve.tensor_tensor(square[:, :, :], xv, xv, ALU.mult))
                link(dve.tensor_reduce(n1_var[:, :], square[:, :, :], AX_X, ALU.add))
                link(dve.tensor_scalar(n1_var[:, :], n1_var[:, :], 1.0 / C, LN_EPS, ALU.mult, ALU.add))

            def norm1_b(b, par):
                xv = xs[:, par]
                dve.wait_ge(n1_rooted, b + 1)
                dve.reciprocal(n1_inv[:, :], n1_root[:, :]).then_inc(n1_step, 1)
                dve.wait_ge(n1_step, N1_STEPS * (b + 1))
                dve.tensor_tensor(xv, xv, n1_inv[:, :].unsqueeze(2).to_broadcast([P, T, C]), ALU.mult).then_inc(out_ready, 1)

            def mix_batch(b, par, spread_before):
                if spread_before:
                    norm1_first(b - 1, 1 - par)
                    norm1_a(b - 1, 1 - par)
                for g in range(G):
                    norm0_a(b, par, g)
                    if g == 0 and spread_before:
                        norm1_b(b - 1, 1 - par)
                    norm0_b(b, par, g)

            dve.memset(ones[:, :], 1.0).then_inc(const_set, 1)
            dve.memset(row_sums[:, :, :], 0.0).then_inc(const_set, 1)
            dve.memset(zero[:, :], 0.0).then_inc(const_set, 1)
            dve.memset(one[:, 0:1], 1.0).then_inc(const_set, 1)
            dve.wait_ge(ident_1, 1)
            dve.tensor_copy(ident_b[:, :], ident[:, :]).then_inc(const_set, 1)
            dve.wait_ge(const_set, 5)
            split = [0]

            def link(ins):
                split[0] += 1
                ins.then_inc(u_split, 1)
                dve.wait_ge(u_split, split[0])

            dve.wait_ge(u_in_done, 16)
            link(dve.tensor_copy(u_part[:, 0], u_in))
            link(dve.tensor_tensor(u_rest, u_in, u_part[:, 0], ALU.subtract))
            link(dve.tensor_copy(u_part[:, 1], u_rest))
            link(dve.tensor_tensor(u_rest2, u_rest, u_part[:, 1], ALU.subtract))
            link(dve.tensor_copy(u_part[:, 2], u_rest2))
            for e in range(2):
                for s, pair in enumerate(PARTS):
                    link(dve.tensor_copy(u_stack[:, e, :, s, :], u_part[:, pair[e]]))
            link(dve.memset(one[:, 0:1], 1.0))
            link(dve.memset(one[:, 0:1], 1.0))
            for e, (ps, to) in enumerate(((ps_a, u_left), (ps_t, u_right))):
                dve.wait_ge(u_turned, e + 1)
                dve.tensor_copy(to[:, :], ps[:, :, :].rearrange("p b n -> p (b n)").bitcast(BF16)).then_inc(u_ready, 1)
            dve.wait_ge(u_ready, 2)

            build(0, 0)
            degrees(0, 0, 0)
            mix_batch(0, 0, False)
            build(1, 1)
            degrees(1, 0, 1)
            with dve.Fori(0, B // 2 - 1) as t:
                mix_batch(2 * t + 1, 1, True)
                build(2 * t + 2, 0)
                degrees(2 * t + 2, t + 1, 0)
                mix_batch(2 * t + 2, 0, True)
                build(2 * t + 3, 1)
                degrees(2 * t + 3, t + 1, 1)
            mix_batch(B - 1, 1, True)
            norm1_first(B - 1, 1)
            norm1_a(B - 1, 1)
            norm1_b(B - 1, 1)


_INS = ["x", "adj", "L0_gnn_U", "L0_gnn_w_scale", "L1_gnn_weight", "L1_gnn_bias"]


def kernel(**inputs):
    import numpy as _np
    import concourse.bacc as _bacc
    from concourse import mybir as _mybir
    from concourse.bass_utils import run_bass_kernel_spmd as _run

    nc = _bacc.Bacc("TRN2", target_bir_lowering=False, num_devices=1)
    arrays, args = {}, []
    for name in _INS:
        a = _np.ascontiguousarray(inputs[name])
        if a.ndim == 0:
            a = a.reshape(1)
        arrays[f"in_{name}"] = a
        args.append(nc.dram_tensor(f"in_{name}", a.shape, _mybir.dt.from_np(a.dtype), kind="ExternalInput").ap())
    out = nc.dram_tensor("out", inputs["x"].shape, F32, kind="ExternalOutput").ap()
    graph_layers(nc, *args, out)
    r = _run(nc, [arrays], core_ids=[0])
    return r.results[0]["out"]
```

```python
from contextlib import ExitStack

import concourse.bass as bass
from concourse import mybir

F32 = mybir.dt.float32
BF16 = mybir.dt.bfloat16
ALU = mybir.AluOpType
ACT = mybir.ActivationFunctionType
AX_X = mybir.AxisListType.X

P = 128
CHUNK = 4
CW = CHUNK * P
DEG_EPS = 1e-12
LN_EPS = 1e-5
LEFT_PARTS = (0, 0, 0, 1, 1, 1, 2, 2)
RIGHT_PARTS = (0, 1, 2, 0, 1, 2, 0, 1)
EARLY = 4
IN_MIX = 4
LEAD = 3
BEHIND = (0, 3, 0, 1, 1, 0, 0, 1, 0, 1, 0, 1, 0, 1, 1, 0, 0, 1, 1, 0, 1, 0, 1, 0, 1, 1, 0, 1, 0, 0, 1, 1, 0, 1, 0, 1, 1, 0, 1, 0)
NEXT_BY = (1, 2, 2)
STORE_AT = 2
BY_ONES = 2
CLEAR_AT = 1
LATE_ROOT = 6
ROOT_AT = 2
GATES = 4
PRODUCT_AT = 3
TURN_OUT_AT = 6

DEG_STEPS = 4
N0_STEPS = 11
N1_STEPS = 8


def build_chunks(T):
    return [(j, g, list(range(CHUNK * g, min(CHUNK * g + CHUNK, j + 1)))) for j in range(T) for g in range(j // CHUNK + 1)]


def mix_steps(T):
    out = []
    for g in range(T // CHUNK):
        blocks = range(CHUNK * g, CHUNK * g + CHUNK)
        rows = [(i, [j for j in blocks if j <= i], [j for j in blocks if j > i]) for i in range(T)]
        rows.sort(key=lambda r: 0 if not r[2] else 1 if not r[1] else 2)
        out.append(rows)
    return out


def window_plan(T, chunks):
    n = IN_MIX + LEAD
    plan = [("piece", IN_MIX), ("piece", IN_MIX + 1), ("turn", 0)] + [("piece", k) for k in range(IN_MIX + 2, n)]
    for c in range(len(chunks)):
        plan.append(("chunk", c))
        for _ in range(BEHIND[c]):
            plan.append(("piece", n))
            n += 1
    return plan, n


def graph_layers(nc, x, adj, u, w_scale, weight, bias, out):
    B, N, C = x.shape
    R = u.shape[1]
    T = N // P
    G = T // CHUNK
    chunks = build_chunks(T)
    NCH = len(chunks)
    mix = mix_steps(T)
    turned = [(g, i, tr) for g in range(G) for i, _, tr in mix[g] if tr]
    NTU = len(turned)
    first_turned = [min(n for n, step in enumerate(turned) if step[0] == g) for g in range(G)]
    spread_order = list(range(EARLY, T)) + list(range(EARLY))
    pieces = [(m, h) for m in spread_order for h in range(G // 2)]
    NP = len(pieces)
    ONES_FROM = T - BY_ONES
    SUMMED = sum(1 for j, g, _ in chunks if 0 < j < ONES_FROM and CHUNK * g < j)
    first_of_row = {}
    for c, (j, _, _) in enumerate(chunks):
        first_of_row.setdefault(j, c)

    adj_rows = adj.rearrange("b (r p) n -> b r p n", p=P)
    x_tiles = x.rearrange("b (t p) c -> b p t c", p=P)
    out_tiles = out.rearrange("b (t p) c -> b p t c", p=P)

    def place(row, par):
        return row if row >= EARLY or par == 0 else T + row

    def loads(row, b, t, n):
        again = row // CHUNK + 1
        return 16 * ((1 + again) * (b if row >= EARLY else t) + (1 if n == 1 else 1 + again))

    with ExitStack() as ctx:
        def sb(name, shape, dt=F32):
            return ctx.enter_context(nc.sbuf_tensor(name, shape, dt))

        def pb(name, shape, dt=F32):
            return ctx.enter_context(nc.psum_tensor(name, shape, dt))

        def sem(name):
            return ctx.enter_context(nc.semaphore(name))

        rows = sb("rows", [P, T + EARLY, N])
        xs = sb("xs", [P, 2, T, C])
        shared = sb("shared", [P, N])
        z = shared[:, 0:T * C].rearrange("p (t c) -> p t c", c=C)
        u_left = sb("u_left", [P, N], BF16)
        u_right = sb("u_right", [P, N], BF16)
        kt_last = sb("kt_last", [P, CW])
        kt = [shared[:, T * C:T * C + CW], shared[:, T * C + CW:T * C + 2 * CW], kt_last[:, :]]
        gate = sb("gate", [P, GATES, CW])
        yt = gate[:, 2:4]
        ut = sb("ut", [P, G // 2, CW])
        sums = sb("sums", [P, CW])
        square = sb("square", [P, T, C])
        part_a = square[:, CHUNK:2 * CHUNK]
        part_b = square[:, 2 * CHUNK:3 * CHUNK]
        ident = sb("ident", [P, P])
        ident_b = sb("ident_b", [P, P], BF16)
        ones = sb("ones", [P, 32])
        weight2 = sb("weight2", [P, P])
        bias_b = sb("bias_b", [P, 1, C])
        scale_b = sb("scale_b", [P, 1])
        row_sums = sb("row_sums", [P, T, G])
        row_sum = sb("row_sum", [P, T])
        deg = sb("deg", [P, T])
        deg_root = sb("deg_root", [P, T])
        d = sb("d", [P, T])
        d_out = sb("d_out", [P, T])
        n0_mean = sb("n0_mean", [P, CHUNK])
        n0_var = sb("n0_var", [P, 2, CHUNK])
        n0_root = sb("n0_root", [P, 2, CHUNK])
        n0_inv = sb("n0_inv", [P, CHUNK])
        n1_mean = sb("n1_mean", [P, T])
        n1_var = sb("n1_var", [P, T])
        n1_root = sb("n1_root", [P, T])
        n1_inv = sb("n1_inv", [P, T])
        one = sb("one", [P, 2])
        zero = sb("zero", [P, 1])

        ps_a = pb("ps_a", [P, 2, CW])
        ps_t = pb("ps_t", [P, 2, CW])
        ps_o = pb("ps_o", [P, 2, CW])
        ps_c = pb("ps_c", [P, CW])
        ps_v = pb("ps_v", [P, CW])

        u_in = rows[:, T + 2, 0:T * R].rearrange("p (t r) -> p t r", r=R)
        u_rest = rows[:, T + 2, 512:512 + T * R].rearrange("p (t r) -> p t r", r=R)
        u_rest2 = rows[:, T + 2, 1024:1024 + T * R].rearrange("p (t r) -> p t r", r=R)
        u_part = rows[:, T + 2, 1536:1536 + 3 * T * R // 2].bitcast(BF16).rearrange("p (s t r) -> p s t r", s=3, r=R)
        u_stack = rows[:, T + 3, :].bitcast(BF16).rearrange("p (e t s r) -> p e t s r", e=2, t=T, r=R)

        adj_in = [sem(f"adj_in{r}") for r in range(T + EARLY)]
        x_in = [sem("x_in0"), sem("x_in1")]
        u_in_done = sem("u_in_done")
        const_in = sem("const_in")
        ident_0 = sem("ident_0")
        ident_1 = sem("ident_1")
        weight_zero = sem("weight_zero")
        const_set = sem("const_set")
        u_split = sem("u_split")
        left_stacked = sem("left_stacked")
        u_turned = sem("u_turned")
        u_ready = sem("u_ready")
        gate_ready = sem("gate_ready")
        gate_done = sem("gate_done")
        flip_ready = sem("flip_ready")
        sum_done = sem("sum_done")
        acc_step = sem("acc_step")
        sums_zero = sem("sums_zero")
        k_done = sem("k_done")
        col_ready = sem("col_ready")
        col_out = sem("col_out")
        col_turned = sem("col_turned")
        deg_step = sem("deg_step")
        root_done = sem("root_done")
        z_ready = sem("z_ready")
        scale_done = sem("scale_done")
        kt_ready = sem("kt_ready")
        kt_done = sem("kt_done")
        kt_used = sem("kt_used")
        y_ready = sem("y_ready")
        y_out = sem("y_out")
        y_turned = sem("y_turned")
        n0_step = sem("n0_step")
        n0_rooted = sem("n0_rooted")
        x1_ready = sem("x1_ready")
        row_used = sem("row_used")
        u_out = sem("u_out")
        half_spread = sem("half_spread")
        o_ready = sem("o_ready")
        o_out = sem("o_out")
        f_ready = sem("f_ready")
        n1_step = sem("n1_step")
        n1_rooted = sem("n1_rooted")
        n1_read = sem("n1_read")
        out_ready = sem("out_ready")
        stored = sem("stored")

        def by_node(a):
            return a.rearrange("q (p t) -> q p t", t=T)

        def by_tile(ps):
            return ps[:, :, :].rearrange("p b n -> p (b n)").bitcast(BF16).rearrange("q (t p) -> q p t", t=T)

        block = ctx.enter_context(nc.Block())

        @block.sync
        def _(sp):
            def load_row(b, t, par, row):
                sp.dma_start(rows[:, place(row, par), :], adj_rows[b, row]).then_inc(adj_in[place(row, par)], 16)

            def store(b, par):
                sp.wait_ge(out_ready, b + 1)
                sp.dma_start(out_tiles[b], xs[:, par]).then_inc(stored, 16)

            def behind_the_mix(b, t, par, spread_before=True, last=False):
                if not last:
                    if spread_before:
                        sp.wait_ge(row_used, T * b)
                    else:
                        sp.wait_ge(u_ready, 2)
                    for row in range(EARLY):
                        load_row(b + 1, t + par, 1 - par, row)
                n = 0
                for g in range(G):
                    if g == STORE_AT and spread_before:
                        store(b - 1, 1 - par)
                    for h in range(g):
                        sp.wait_ge(kt_ready, NTU * b + first_turned[g] + CHUNK * (h + 1))
                        for row in range(CHUNK * g, CHUNK * g + CHUNK):
                            load_again(b, par, row, CHUNK * h, CHUNK * (h + 1))
                        while g == G - 1 and not last and n < NEXT_BY[h]:
                            load_next(b, t, par, n)
                            n += 1
                    sp.wait_ge(y_ready, G * b + g + 1)
                    for row in range(CHUNK * g, CHUNK * g + CHUNK):
                        load_again(b, par, row, CHUNK * g, row + 1)

            def load_again(b, par, row, lo, hi):
                sp.dma_start(rows[:, place(row, par), lo * P:hi * P], adj_rows[b, row][:, lo * P:hi * P]).then_inc(
                    adj_in[place(row, par)], 16)

            def load_next(b, t, par, n):
                sp.wait_ge(row_used, T * b + n + 1)
                load_row(b + 1, t + par, 1 - par, spread_order[n])

            def behind_the_spread(b, t, par, spread_before=True):
                for n in range(NEXT_BY[-1], T - EARLY):
                    load_next(b, t, par, n)
                if spread_before:
                    sp.wait_ge(stored, 16 * b)
                sp.dma_start(xs[:, 1 - par], x_tiles[b + 1]).then_inc(x_in[1 - par], 16)

            sp.dma_start(u_in, u.rearrange("(p t) r -> p t r", p=P)).then_inc(u_in_done, 16)
            for row in range(T):
                load_row(0, 0, 0, row)
            sp.dma_start(xs[:, 0], x_tiles[0]).then_inc(x_in[0], 16)
            behind_the_mix(0, 0, 0, spread_before=False)
            behind_the_spread(0, 0, 0, spread_before=False)
            with sp.Fori(0, B // 2 - 1) as t:
                behind_the_mix(2 * t + 1, t, 1)
                behind_the_spread(2 * t + 1, t, 1)
                behind_the_mix(2 * t + 2, t + 1, 0)
                behind_the_spread(2 * t + 2, t + 1, 0)
            behind_the_mix(B - 1, B // 2 - 1, 1, last=True)
            for h in range(G // 2):
                tiles = slice(h * T // 2, (h + 1) * T // 2)
                sp.wait_ge(out_ready, B + h)
                sp.dma_start(out_tiles[B - 1][:, tiles], xs[:, 0, tiles]).then_inc(stored, 16)
            sp.wait_ge(stored, 16 * (B + 1))

        @block.gpsimd
        def _(pool):
            pool.memset(ident[:, :], 0.0).then_inc(ident_0, 1)
            pool.wait_ge(ident_0, 1)
            pool.affine_select(out=ident[:, :], in_=ident[:, :], compare_op=ALU.not_equal, fill=1.0, base=0,
                               pattern=[[-1, P]], channel_multiplier=1).then_inc(ident_1, 1)

            def column_sums(b, par):
                base = SUMMED * b
                pool.wait_ge(sums_zero, b + 1)
                n = 0
                for c, (j, g, blocks) in enumerate(chunks):
                    w = P * len([i for i in blocks if i < j])
                    if j >= ONES_FROM or not w:
                        continue
                    pool.wait_ge(k_done, NCH * b + c + 1)
                    if n:
                        pool.wait_ge(acc_step, base + n)
                    acc = shared[:, g * CW:g * CW + w]
                    pool.tensor_tensor(acc, acc, rows[:, place(j, par), g * CW:g * CW + w], ALU.add).then_inc(acc_step, 1)
                    n += 1

            column_sums(0, 0)
            column_sums(1, 1)
            with pool.Fori(0, B // 2 - 1) as t:
                column_sums(2 * t + 2, 0)
                column_sums(2 * t + 3, 1)

        @block.tensor
        def _(pe):
            def build_chunk(b, t, par, c):
                j, g, blocks = chunks[c]
                w = P * len(blocks)
                buf = c % 2
                if c < 2:
                    if not (isinstance(b, int) and b == 0):
                        pe.wait_ge(y_out, G * b)
                else:
                    pe.wait_ge(gate_done, NCH * b + c - 1)
                pe.matmul(ps_a[:, buf, 0:w], u_left[:, j * P:(j + 1) * P], u_right[:, g * CW:g * CW + w],
                          start=True, stop=True).then_inc(gate_ready, 1)
                if first_of_row[j] == c:
                    pe.wait_ge(adj_in[place(j, par)], loads(j, b, t, 1))
                if c >= 2:
                    pe.wait_ge(sum_done, NCH * b + c - 1)
                for k, i in enumerate(blocks):
                    last = pe.transpose(ps_t[:, buf, k * P:(k + 1) * P],
                                        rows[:, place(i, par), j * P:(j + 1) * P], ident[:, :])
                last.then_inc(flip_ready, 1)

            def column_sums(b, par, j):
                if j == ONES_FROM:
                    pe.wait_ge(acc_step, SUMMED * (b + 1))
                    for g in range(G):
                        pe.matmul(ps_c[32 * g:32 * g + 32, :], ones[:, :], shared[:, g * CW:(g + 1) * CW],
                                  start=True, stop=False, skip_group_check=True)
                for g in range(G):
                    w = min(CW, (j - CHUNK * g) * P)
                    pe.wait_ge(k_done, NCH * b + first_of_row[j] + g + 1)
                    last = pe.matmul(ps_c[32 * g:32 * g + 32, 0:w], ones[:, :],
                                     rows[:, place(j, par), g * CW:g * CW + w],
                                     start=False, stop=(j == T - 1), skip_group_check=True)
                if j == T - 1:
                    last.then_inc(col_ready, 1)

            def turn_sums(b):
                pe.wait_ge(col_out, b + 1)
                if not (isinstance(b, int) and b == 0):
                    pe.wait_ge(n0_step, N0_STEPS * G * b)
                for k in range(CHUNK):
                    last = pe.transpose(ps_v[:, k * P:(k + 1) * P], sums[:, k * P:(k + 1) * P], ident[:, :])
                last.then_inc(col_turned, 1)

            def turn_k(b, par, n):
                g, i, tr = turned[n]
                if n < 2:
                    pe.wait_ge(k_done, NCH * b + NCH)
                else:
                    pe.wait_ge(kt_done, NTU * b + n - 1)
                for j in tr:
                    k = j - CHUNK * g
                    last = pe.transpose(ps_t[:, n % 2, k * P:(k + 1) * P],
                                        rows[:, place(j, par), i * P:(i + 1) * P], ident[:, :])
                last.then_inc(kt_ready, 1)

            def mix_batch(b, t, par, spread_before):
                n, half = 0, 0
                for g in range(G):
                    if g >= 2:
                        pe.wait_ge(y_out, G * b + g - 1)
                    started = [False, False]
                    for s, (i, nat, tr) in enumerate(mix[g]):
                        if g == 0:
                            pe.wait_ge(z_ready, G * b + i // CHUNK + 1)
                        parts = []
                        if tr:
                            lo = tr[0] - CHUNK * g
                            if n + 2 < NTU:
                                turn_k(b, par, n + 2)
                            parts.append((lo, len(tr), kt[n % 3][:, lo * P:(lo + len(tr)) * P], n))
                            n += 1
                        if nat:
                            lo = nat[0] - CHUNK * g
                            parts.append((lo, len(nat), rows[:, place(i, par), nat[0] * P:(nat[-1] + 1) * P], None))
                        for lo, k, moving, item in parts:
                            if item is not None:
                                pe.wait_ge(kt_done, NTU * b + item + 1)
                            assert started[half] or k == CHUNK
                            last = pe.matmul(ps_a[C * half:C * half + C, g % 2, lo * P:(lo + k) * P], z[:, i], moving,
                                             start=not started[half], stop=True, skip_group_check=True)
                            started[half] = True
                            half = 1 - half
                            if item is not None:
                                last.then_inc(kt_used, 1)
                        if s == 1 and g >= 1:
                            turn_y(b, g - 1)
                        if g == G - 1 and 2 <= s < IN_MIX + 2:
                            piece(b, t, par, s - 2)
                        if g == 0 and spread_before and s in (PRODUCT_AT, TURN_OUT_AT):
                            for h in range(G // 2):
                                (times_weight if s == PRODUCT_AT else turn_out)(b - 1, h)
                    last.then_inc(y_ready, 1)

            def turn_y(b, g):
                pe.wait_ge(y_out, G * b + g + 1)
                if g == 0:
                    pe.wait_ge(scale_done, b + 1)
                else:
                    pe.wait_ge(n0_step, N0_STEPS * (G * b + g))
                for k in range(CHUNK):
                    last = pe.transpose(ps_v[:, k * P:(k + 1) * P], yt[:, g % 2, k * P:(k + 1) * P], ident[:, :])
                last.then_inc(y_turned, 1)

            def piece(b, t, par, n):
                m, h = pieces[n]
                if n == 0 and not (isinstance(b, int) and b == 0):
                    pe.wait_ge(n1_read, 2 * b)
                if h == 0 or (isinstance(b, int) and b == B - 1):
                    pe.wait_ge(x1_ready, G * b + m // CHUNK + 1)
                    pe.wait_ge(adj_in[place(m, par)], loads(m, b, t, 2))
                for q in range(2):
                    g = 2 * h + q
                    last = pe.matmul(ps_o[C * q:C * q + C, h, :], xs[:, par, m, :],
                                     rows[:, place(m, par), g * CW:(g + 1) * CW],
                                     start=(m == spread_order[0]), stop=(m == spread_order[-1]), skip_group_check=True)
                if isinstance(b, int) and b == B - 1 and m == spread_order[-1]:
                    last.then_inc(half_spread, 1)
                elif h == G // 2 - 1:
                    last.then_inc(row_used, 1)

            def times_weight(b, h):
                pe.wait_ge(u_out, 2 * b + h + 1)
                pe.wait_ge(const_in, 64)
                pe.matmul(ps_o[:, h, :], weight2[:, :], ut[:, h, :], start=True, stop=True,
                          skip_group_check=True).then_inc(o_ready, 1)

            def turn_out(b, h):
                pe.wait_ge(o_out, 2 * b + h + 1)
                for k in range(CHUNK):
                    last = pe.transpose(ps_o[:, h, k * P:(k + 1) * P], ut[:, h, k * P:(k + 1) * P], ident[:, :])
                last.then_inc(f_ready, 1)

            plan, planned = window_plan(T, chunks)

            def window(b, t, par):
                for what, n in plan:
                    if what == "piece":
                        piece(b, t, par, n)
                    elif what == "turn":
                        turn_y(b, G - 1)
                    else:
                        build_chunk(b + 1, t + par, 1 - par, n)
                close_build(b + 1, 1 - par)
                for n in range(planned, NP):
                    piece(b, t, par, n)

            def close_build(b, par):
                for j in range(ONES_FROM, T):
                    column_sums(b, par, j)
                turn_k(b, par, 0)
                turn_k(b, par, 1)
                turn_sums(b)

            pe.wait_ge(const_set, 5)
            pe.wait_ge(left_stacked, 3)
            for e, ps in enumerate((ps_a, ps_t)):
                target = ps[:, :, :].rearrange("p b n -> p (b n)").bitcast(BF16)
                if e == 1:
                    pe.wait_ge(u_split, 5 + 3)
                for tt in range(T):
                    last = pe.transpose(target[:, tt * P:(tt + 1) * P],
                                        u_stack[:, e, tt].rearrange("p s r -> p (s r)"), ident_b[:, :])
                last.then_inc(u_turned, 1)
            pe.wait_ge(u_ready, 2)
            pe.wait_ge(ident_1, 1)
            for c in range(NCH):
                build_chunk(0, 0, 0, c)
            close_build(0, 0)
            mix_batch(0, 0, 0, False)
            window(0, 0, 0)
            with pe.Fori(0, B // 2 - 1) as t:
                mix_batch(2 * t + 1, t, 1, True)
                window(2 * t + 1, t, 1)
                mix_batch(2 * t + 2, t + 1, 0, True)
                window(2 * t + 2, t + 1, 0)
            mix_batch(B - 1, B // 2 - 1, 1, True)
            for h in range(G // 2):
                for k, n in enumerate(range(IN_MIX + h, NP, 2)):
                    piece(B - 1, B // 2 - 1, 1, n)
                    if k == 1 and h == 0:
                        turn_y(B - 1, G - 1)
                    if k == 1 and h == 1:
                        times_weight(B - 1, 0)
                    if k == 3 and h == 1:
                        turn_out(B - 1, 0)
            times_weight(B - 1, 1)
            turn_out(B - 1, 1)

        @block.scalar
        def _(act):
            def gates(b, spread):
                for c, (j, g, blocks) in enumerate(chunks):
                    w = P * len(blocks)
                    act.wait_ge(gate_ready, NCH * b + c + 1)
                    if c >= GATES:
                        act.wait_ge(k_done, NCH * b + c + 1 - GATES)
                    elif c == 2 and spread:
                        act.wait_ge(y_turned, G * b)
                    act.activation(gate[:, c % GATES, 0:w], ps_a[:, c % 2, 0:w], ACT.Sigmoid).then_inc(gate_done, 1)
                    if c == CLEAR_AT and spread:
                        clear_sums()
                    if c == ROOT_AT and spread:
                        root_n0(b - 1, G - 1)

            def degrees(b):
                act.activation(one[:, 1:2], one[:, 0:1], ACT.Sqrt)
                act.wait_ge(col_ready, b + 1)
                act.copy(sums[:, :], ps_c[:, :]).then_inc(col_out, 1)
                act.wait_ge(deg_step, DEG_STEPS * b + 3)
                act.activation(deg_root[:, :], deg[:, :], ACT.Sqrt).then_inc(root_done, 1)

            def spread_out(b):
                act.wait_ge(row_used, T * b + T)
                for h in range(G // 2):
                    act.copy(ut[:, h, :], ps_o[:, h, :]).then_inc(u_out, 1)

            def root_n0(b, g):
                act.wait_ge(n0_step, N0_STEPS * (G * b + g) + 10)
                act.activation(n0_root[:, g % 2, :], n0_var[:, g % 2, :], ACT.Sqrt).then_inc(n0_rooted, 1)

            def leave_out(b, h):
                act.wait_ge(o_ready, 2 * b + h + 1)
                act.copy(ut[:, h, :], ps_o[:, h, :]).then_inc(o_out, 1)

            def root_n1(run, tiles):
                act.wait_ge(n1_step, N1_STEPS * run + 7)
                act.activation(n1_root[:, tiles], n1_var[:, tiles], ACT.Sqrt).then_inc(n1_rooted, 1)

            def mix_batch(b, spread_before):
                def turn(n):
                    g, i, tr = turned[n]
                    lo, w = (tr[0] - CHUNK * g) * P, len(tr) * P
                    act.wait_ge(kt_ready, NTU * b + n + 1)
                    if n >= 3:
                        act.wait_ge(kt_used, NTU * b + n - 2)
                    act.copy(kt[n % 3][:, lo:lo + w], ps_t[:, n % 2, lo:lo + w]).then_inc(kt_done, 1)

                def leave(g):
                    act.wait_ge(y_ready, G * b + g + 1)
                    act.copy(yt[:, g % 2, :], ps_a[:, g % 2, :]).then_inc(y_out, 1)

                for n in range(NTU):
                    turn(n)
                    if n == 1 and spread_before:
                        for h in range(G // 2):
                            leave_out(b - 1, h)
                    for g in range(1, G):
                        if n == first_turned[g] + 1:
                            leave(g - 1)
                    if n == first_turned[1] + 5:
                        if spread_before:
                            root_n1(b - 1, slice(0, T))
                        root_n0(b, 0)
                    if n == first_turned[2] + 8:
                        root_n0(b, 1)
                    if n == first_turned[3] + LATE_ROOT:
                        root_n0(b, 2)
                leave(G - 1)

            def clear_sums():
                act.copy(shared[:, :], zero[:, :].to_broadcast([P, N])).then_inc(sums_zero, 1)

            def build(b, spread=True):
                gates(b, spread)
                degrees(b)

            act.wait_ge(weight_zero, 1)
            for q in range(2):
                half = slice(C * q, C * q + C)
                act.dma_start(weight2[half, half], weight).then_inc(const_in, 16)
            act.dma_start(bias_b[:, 0, :], bias.partition_broadcast(P)).then_inc(const_in, 16)
            act.dma_start(scale_b[:, :], w_scale.partition_broadcast(P)).then_inc(const_in, 16)
            act.wait_ge(u_split, 5)
            for part in range(3):
                slots = [s for s in range(len(LEFT_PARTS)) if LEFT_PARTS[s] == part]
                act.copy(u_stack[:, 0, :, slots[0]:slots[-1] + 1, :],
                         u_part[:, part].unsqueeze(2).to_broadcast([P, T, len(slots), R])).then_inc(left_stacked, 1)
            act.wait_ge(u_turned, 1)
            act.copy(by_node(u_left[:, :]), by_tile(ps_a)).then_inc(u_ready, 1)
            act.wait_ge(const_set, 5)
            clear_sums()
            build(0, spread=False)
            mix_batch(0, False)
            build(1)
            spread_out(0)
            with act.Fori(0, B // 2 - 1) as t:
                mix_batch(2 * t + 1, True)
                build(2 * t + 2)
                spread_out(2 * t + 1)
                mix_batch(2 * t + 2, True)
                build(2 * t + 3)
                spread_out(2 * t + 2)
            mix_batch(B - 1, True)
            root_n0(B - 1, G - 1)
            for h in range(G // 2):
                act.wait_ge(half_spread, h + 1)
                act.copy(ut[:, h, :], ps_o[:, h, :]).then_inc(u_out, 1)
                leave_out(B - 1, h)
                root_n1(B - 1 + h, slice(h * T // 2, (h + 1) * T // 2))

        @block.vector
        def _(dve):
            def build(b, par, spread=True):
                def add(c):
                    j, g, blocks = chunks[c]
                    w = P * len(blocks)
                    k = rows[:, place(j, par), g * CW:g * CW + w]
                    dve.wait_ge(flip_ready, NCH * b + c + 1)
                    dve.tensor_tensor(k, k, ps_t[:, c % 2, 0:w], ALU.add).then_inc(sum_done, 1)

                def multiply(c):
                    j, g, blocks = chunks[c]
                    w = P * len(blocks)
                    k = rows[:, place(j, par), g * CW:g * CW + w]
                    dve.wait_ge(gate_done, NCH * b + c + 1)
                    dve.wait_ge(sum_done, NCH * b + c + 1)
                    dve.scalar_tensor_tensor(k, k, 1.0, gate[:, c % GATES, 0:w], ALU.mult, ALU.mult,
                                             accum_out=row_sums[:, j, g:g + 1]).then_inc(k_done, 1)

                for c in range(NCH):
                    if c == 0:
                        add(c)
                    if c + 1 < NCH:
                        add(c + 1)
                    multiply(c)
                    if c == ROOT_AT and spread:
                        norm0_b(b - 1, 1 - par, G - 1)

            def degrees(b, t, par):
                base = DEG_STEPS * b
                dve.wait_ge(k_done, NCH * b + NCH)
                dve.tensor_reduce(row_sum[:, :], row_sums[:, :, :], AX_X, ALU.add).then_inc(deg_step, 1)
                dve.wait_ge(deg_step, base + 1)
                dve.wait_ge(col_turned, b + 1)
                col = ps_v[:, :].rearrange("p (k g r) -> p g k r", k=CHUNK, r=32)[:, :, :, 0]
                dve.tensor_tensor(deg[:, :].rearrange("p (g k) -> p g k", k=CHUNK),
                                  row_sum[:, :].rearrange("p (g k) -> p g k", k=CHUNK), col, ALU.add).then_inc(deg_step, 1)
                dve.wait_ge(deg_step, base + 2)
                dve.tensor_scalar(deg[:, :], deg[:, :], 0.5, DEG_EPS, ALU.mult, ALU.max).then_inc(deg_step, 1)
                dve.wait_ge(root_done, b + 1)
                dve.reciprocal(d[:, :], deg_root[:, :]).then_inc(deg_step, 1)
                dve.wait_ge(deg_step, base + 4)
                dve.wait_ge(x_in[par], 16 * t + 16)
                for g in range(G):
                    s = slice(CHUNK * g, CHUNK * g + CHUNK)
                    dve.tensor_tensor(z[:, s, :], xs[:, par, s, :],
                                      d[:, s].unsqueeze(2).to_broadcast([P, CHUNK, C]), ALU.mult).then_inc(z_ready, 1)
                dve.wait_ge(const_in, 64)
                dve.tensor_scalar(d_out[:, :], d[:, :], scale_b[:, 0:1], 0.5, ALU.mult, ALU.mult).then_inc(scale_done, 1)
                dve.wait_ge(scale_done, b + 1)

            def norm0_a(b, par, g):
                base = N0_STEPS * (G * b + g)
                step = [0]

                def link(ins):
                    step[0] += 1
                    ins.then_inc(n0_step, 1)
                    dve.wait_ge(n0_step, base + step[0])

                s = slice(CHUNK * g, CHUNK * g + CHUNK)
                xv = xs[:, par, s, :]
                y = ps_v[:, :].rearrange("p (k h c) -> p k h c", k=CHUNK, h=2)
                dv = d_out[:, s].unsqueeze(2).to_broadcast([P, CHUNK, C])
                sq = square[:, 0:CHUNK]
                dve.wait_ge(y_turned, G * b + g + 1)
                link(dve.tensor_tensor(part_a, y[:, :, 0, :], dv, ALU.mult))
                link(dve.tensor_tensor(part_b, y[:, :, 1, :], dv, ALU.mult))
                link(dve.tensor_tensor(part_a, part_a, part_b, ALU.add))
                link(dve.tensor_tensor(xv, xv, part_a, ALU.add))
                link(dve.tensor_reduce(n0_mean[:, :], xv, AX_X, ALU.add))
                link(dve.tensor_scalar(n0_mean[:, :], n0_mean[:, :], 1.0 / C, None, ALU.mult))
                link(dve.tensor_tensor(xv, xv, n0_mean[:, :].unsqueeze(2).to_broadcast([P, CHUNK, C]), ALU.subtract))
                link(dve.tensor_tensor(sq, xv, xv, ALU.mult))
                link(dve.tensor_reduce(n0_var[:, g % 2, :], sq, AX_X, ALU.add))
                link(dve.tensor_scalar(n0_var[:, g % 2, :], n0_var[:, g % 2, :], 1.0 / C, LN_EPS, ALU.mult, ALU.add))

            def norm0_b(b, par, g):
                s = slice(CHUNK * g, CHUNK * g + CHUNK)
                xv = xs[:, par, s, :]
                dve.wait_ge(n0_rooted, G * b + g + 1)
                dve.reciprocal(n0_inv[:, :], n0_root[:, g % 2, :]).then_inc(n0_step, 1)
                dve.wait_ge(n0_step, N0_STEPS * (G * b + g + 1))
                dve.tensor_tensor(xv, xv, n0_inv[:, :].unsqueeze(2).to_broadcast([P, CHUNK, C]),
                                  ALU.mult).then_inc(x1_ready, 1)
                dve.wait_ge(x1_ready, G * b + g + 1)

            def norm1_first(b, par, h, to):
                dve.wait_ge(f_ready, 2 * b + h + 1)
                x1, s = [xs[:, v, h * T // 2:(h + 1) * T // 2, :].rearrange("p (q k) c -> p k q c", k=CHUNK)
                         for v in (par, to)]
                f = ps_o[:, h, :].rearrange("p (k q c) -> p k q c", k=CHUNK, c=C)
                dve.tensor_tensor(s, x1, f, ALU.add).then_inc(n1_read, 1)
                dve.wait_ge(n1_read, 2 * b + h + 1)

            def norm1_a(run, par, tiles):
                step = [0]
                size = tiles.stop - tiles.start

                def link(ins):
                    step[0] += 1
                    ins.then_inc(n1_step, 1)
                    dve.wait_ge(n1_step, N1_STEPS * run + step[0])

                xv = xs[:, par, tiles]
                mean, var, sq = n1_mean[:, tiles], n1_var[:, tiles], square[:, tiles]
                link(dve.tensor_tensor(xv, xv, bias_b[:, :, :].to_broadcast([P, size, C]), ALU.add))
                link(dve.tensor_reduce(mean, xv, AX_X, ALU.add))
                link(dve.tensor_scalar(mean, mean, 1.0 / C, None, ALU.mult))
                link(dve.tensor_tensor(xv, xv, mean.unsqueeze(2).to_broadcast([P, size, C]), ALU.subtract))
                link(dve.tensor_tensor(sq, xv, xv, ALU.mult))
                link(dve.tensor_reduce(var, sq, AX_X, ALU.add))
                link(dve.tensor_scalar(var, var, 1.0 / C, LN_EPS, ALU.mult, ALU.add))

            def norm1_b(run, par, tiles):
                size = tiles.stop - tiles.start
                xv = xs[:, par, tiles]
                dve.wait_ge(n1_rooted, run + 1)
                dve.reciprocal(n1_inv[:, tiles], n1_root[:, tiles]).then_inc(n1_step, 1)
                dve.wait_ge(n1_step, N1_STEPS * (run + 1))
                dve.tensor_tensor(xv, xv, n1_inv[:, tiles].unsqueeze(2).to_broadcast([P, size, C]),
                                  ALU.mult).then_inc(out_ready, 1)

            def mix_batch(b, par, spread_before):
                if spread_before:
                    for h in range(G // 2):
                        norm1_first(b - 1, 1 - par, h, 1 - par)
                    norm1_a(b - 1, 1 - par, slice(0, T))
                for g in range(G):
                    norm0_a(b, par, g)
                    if g == 0 and spread_before:
                        norm1_b(b - 1, 1 - par, slice(0, T))
                    if g < G - 1:
                        norm0_b(b, par, g)

            dve.memset(weight2[:, :], 0.0).then_inc(weight_zero, 1)
            dve.memset(ones[:, :], 1.0).then_inc(const_set, 1)
            dve.memset(row_sums[:, :, :], 0.0).then_inc(const_set, 1)
            dve.memset(zero[:, :], 0.0).then_inc(const_set, 1)
            dve.memset(one[:, 0:1], 1.0).then_inc(const_set, 1)
            dve.wait_ge(ident_1, 1)
            dve.tensor_copy(ident_b[:, :], ident[:, :]).then_inc(const_set, 1)
            dve.wait_ge(const_set, 5)
            split = [0]

            def link(ins):
                split[0] += 1
                ins.then_inc(u_split, 1)
                dve.wait_ge(u_split, split[0])

            dve.wait_ge(u_in_done, 16)
            link(dve.tensor_copy(u_part[:, 0], u_in))
            link(dve.tensor_tensor(u_rest, u_in, u_part[:, 0], ALU.subtract))
            link(dve.tensor_copy(u_part[:, 1], u_rest))
            link(dve.tensor_tensor(u_rest2, u_rest, u_part[:, 1], ALU.subtract))
            link(dve.tensor_copy(u_part[:, 2], u_rest2))
            for lo in range(0, len(RIGHT_PARTS), 3):
                hi = min(lo + 3, len(RIGHT_PARTS))
                link(dve.tensor_copy(u_stack[:, 1, :, lo:hi, :],
                                     u_part[:, 0:hi - lo].rearrange("p s t r -> p t s r")))
            dve.wait_ge(u_turned, 2)
            dve.tensor_copy(by_node(u_right[:, :]), by_tile(ps_t)).then_inc(u_ready, 1)
            dve.wait_ge(u_ready, 2)

            build(0, 0, spread=False)
            degrees(0, 0, 0)
            mix_batch(0, 0, False)
            build(1, 1)
            degrees(1, 0, 1)
            with dve.Fori(0, B // 2 - 1) as t:
                mix_batch(2 * t + 1, 1, True)
                build(2 * t + 2, 0)
                degrees(2 * t + 2, t + 1, 0)
                mix_batch(2 * t + 2, 0, True)
                build(2 * t + 3, 1)
                degrees(2 * t + 3, t + 1, 1)
            mix_batch(B - 1, 1, True)
            norm0_b(B - 1, 1, G - 1)
            dve.wait_ge(stored, 16 * (B - 1))
            for h in range(G // 2):
                tiles = slice(h * T // 2, (h + 1) * T // 2)
                norm1_first(B - 1, 1, h, 0)
                norm1_a(B - 1 + h, 0, tiles)
                norm1_b(B - 1 + h, 0, tiles)


_INS = ["x", "adj", "L0_gnn_U", "L0_gnn_w_scale", "L1_gnn_weight", "L1_gnn_bias"]


def kernel(**inputs):
    import numpy as _np
    import concourse.bacc as _bacc
    from concourse import mybir as _mybir
    from concourse.bass_utils import run_bass_kernel_spmd as _run

    nc = _bacc.Bacc("TRN2", target_bir_lowering=False, num_devices=1)
    arrays, args = {}, []
    for name in _INS:
        a = _np.ascontiguousarray(inputs[name])
        if a.ndim == 0:
            a = a.reshape(1)
        arrays[f"in_{name}"] = a
        args.append(nc.dram_tensor(f"in_{name}", a.shape, _mybir.dt.from_np(a.dtype), kind="ExternalInput").ap())
    out = nc.dram_tensor("out", inputs["x"].shape, F32, kind="ExternalOutput").ap()
    graph_layers(nc, *args, out)
    r = _run(nc, [arrays], core_ids=[0])
    return r.results[0]["out"]
```
